# Optimizing a Trainium2 kernel written in Bass

```python
import numpy as np
import jax
import jax.numpy as jnp

def _softmax(x, axis=-1):
    return jax.nn.softmax(x, axis=axis)

def _gelu(x):
    return jax.nn.gelu(x, approximate=True)

def _silu(x):
    return jax.nn.silu(x)

def _sigmoid(x):
    return jax.nn.sigmoid(x)

def _layernorm(x, axis=-1, eps=1e-05):
    m = jnp.mean(x, axis=axis, keepdims=True)
    v = jnp.var(x, axis=axis, keepdims=True)
    return (x - m) / jnp.sqrt(v + eps)

def _scatter_add(tgt, idx, src, axis=0):
    return tgt.at[idx].add(src)

def _segment_sum(src, seg, n):
    return jax.ops.segment_sum(src, seg, n)
kernel_name = 'mk_prb_d1_jaxref_r2_dfc1ee'

def setup_inputs(seed: int=0):
    np.random.seed(seed)
    _w = jnp.asarray

    def _L0_attn_setup():
        import jax, jax.numpy as jnp
        import numpy as np
        import math
        NUM_RFS = 512
        DIM = 512
        OUT_DIM = 512
        B, S = (4, 1024)

        def _rfs(xw, ab, AB, gs):
            dot_products = jnp.einsum('...d,rd->...r', xw, ab[:, None] * gs)
            correction = (0.5 * jnp.sum(xw * xw, axis=-1))[..., None] * (ab * ab)
            return 1.0 / math.sqrt(NUM_RFS) * AB * jnp.exp(dot_products - correction)
        key = jax.random.key(seed)
        k1, k2, k3, k4 = jax.random.split(key, 4)
        x = jax.random.normal(k1, (B, S, DIM), dtype=jnp.float32) * 0.03
        input_weights = jax.random.normal(k2, (OUT_DIM, DIM), dtype=jnp.float32) * 0.03
        xis = jax.random.uniform(k3, (NUM_RFS,), dtype=jnp.float32) * 0.5
        proj_matrix = jax.random.normal(k4, (NUM_RFS, DIM), dtype=jnp.float32)
        return {'x': x, 'input_weights': input_weights, 'xis': xis, 'proj_matrix': proj_matrix}
    _L0_attn_in = _L0_attn_setup()

    def _L0_ffn_setup():
        import jax, jax.numpy as jnp
        import numpy as np
        B, S, H = (2, 256, 512)
        E, I = (64, 256)
        K = 8
        G, TG = (8, 4)
        SCALE = 2.5
        T = B * S
        CAP = 256

        def _moe_forward(x, router_w, gate_w, up_w, down_w, shared_gate_w, shared_up_w, shared_down_w):
            b, s, h = x.shape
            tokens = x.reshape(-1, h)
            t = tokens.shape[0]
            logits = tokens @ router_w
            scores = jax.nn.sigmoid(logits)
            eg = E // G
            group_scores = scores.reshape(t, G, eg).max(axis=-1)
            _, sel_groups = jax.lax.top_k(group_scores, TG)
            group_mask = jnp.zeros((t, G), bool).at[jnp.arange(t)[:, None], sel_groups].set(True)
            expert_mask = jnp.repeat(group_mask, eg, axis=1)
            masked_scores = jnp.where(expert_mask, scores, 0.0)
            topk_w, topk_idx = jax.lax.top_k(masked_scores, K)
            topk_w = topk_w / jnp.clip(topk_w.sum(-1, keepdims=True), 1e-09)
            topk_w = topk_w * SCALE
            flat_e = topk_idx.reshape(-1)
            onehot = jax.nn.one_hot(flat_e, E, dtype=jnp.int32)
            prior = jnp.cumsum(onehot, axis=0) - onehot
            pos = jnp.take_along_axis(prior, flat_e[:, None], axis=1)[:, 0]
            valid = (pos < CAP).astype(tokens.dtype)
            pos_c = jnp.minimum(pos, CAP - 1)
            tidx = jnp.repeat(jnp.arange(t), K)
            dispatch = jnp.zeros((E, CAP, h), tokens.dtype)
            dispatch = dispatch.at[flat_e, pos_c].add(tokens[tidx] * valid[:, None])
            g = jnp.einsum('ech,ehi->eci', dispatch, gate_w)
            u = jnp.einsum('ech,ehi->eci', dispatch, up_w)
            expert_out = jnp.einsum('eci,eih->ech', jax.nn.silu(g) * u, down_w)
            gathered = expert_out[flat_e, pos_c]
            contrib = gathered * (topk_w.reshape(-1) * valid)[:, None]
            output = jnp.zeros((t, h), tokens.dtype).at[tidx].add(contrib)
            sg = jax.nn.silu(tokens @ shared_gate_w) * (tokens @ shared_up_w)
            output = output + sg @ shared_down_w
            return output.reshape(b, s, h)
        key = jax.random.key(seed)
        ks = jax.random.split(key, 9)
        s_h = 1.0 / np.sqrt(H)
        s_i = 1.0 / np.sqrt(I)
        return {'x': jax.random.normal(ks[0], (B, S, H), jnp.float32), 'router_w': jax.random.normal(ks[1], (H, E), jnp.float32) * s_h, 'gate_w': jax.random.normal(ks[2], (E, H, I), jnp.float32) * s_h, 'up_w': jax.random.normal(ks[3], (E, H, I), jnp.float32) * s_h, 'down_w': jax.random.normal(ks[4], (E, I, H), jnp.float32) * s_i, 'shared_gate_w': jax.random.normal(ks[5], (H, I), jnp.float32) * s_h, 'shared_up_w': jax.random.normal(ks[6], (H, I), jnp.float32) * s_h, 'shared_down_w': jax.random.normal(ks[7], (I, H), jnp.float32) * s_i}
    _L0_ffn_in = _L0_ffn_setup()
    _d = {'L0_attn_x': _L0_attn_in['x'], 'L0_attn_input_weights': _L0_attn_in['input_weights'], 'L0_attn_xis': _L0_attn_in['xis'], 'L0_attn_proj_matrix': _L0_attn_in['proj_matrix'], 'L0_ffn_router_w': _L0_ffn_in['router_w'], 'L0_ffn_gate_w': _L0_ffn_in['gate_w'], 'L0_ffn_up_w': _L0_ffn_in['up_w'], 'L0_ffn_down_w': _L0_ffn_in['down_w'], 'L0_ffn_shared_gate_w': _L0_ffn_in['shared_gate_w'], 'L0_ffn_shared_up_w': _L0_ffn_in['shared_up_w'], 'L0_ffn_shared_down_w': _L0_ffn_in['shared_down_w']}
    _x0 = _d['L0_attn_x']
    _d['L0_attn_x'] = jax.random.normal(jax.random.fold_in(jax.random.key(seed), 1), (4, 2048, 512), dtype=_x0.dtype)
    del _x0
    return _d

def reference(L0_attn_x, L0_attn_input_weights, L0_attn_xis, L0_attn_proj_matrix, L0_ffn_router_w, L0_ffn_gate_w, L0_ffn_up_w, L0_ffn_down_w, L0_ffn_shared_gate_w, L0_ffn_shared_up_w, L0_ffn_shared_down_w):

    def _L0_attn_ref(x, input_weights, xis, proj_matrix):
        import jax, jax.numpy as jnp
        import numpy as np
        import math
        NUM_RFS = 512
        DIM = 512
        OUT_DIM = 512
        B, S = (4, 1024)

        def _rfs(xw, ab, AB, gs):
            dot_products = jnp.einsum('...d,rd->...r', xw, ab[:, None] * gs)
            correction = (0.5 * jnp.sum(xw * xw, axis=-1))[..., None] * (ab * ab)
            return 1.0 / math.sqrt(NUM_RFS) * AB * jnp.exp(dot_products - correction)
        ab = xis
        AB = jnp.exp(xis)
        weights = _rfs(input_weights, ab, AB, proj_matrix)
        feats = _rfs(x, ab, AB, proj_matrix)
        return jnp.einsum('bsr,or->bso', feats, weights)

    def _L0_ffn_ref(x, router_w, gate_w, up_w, down_w, shared_gate_w, shared_up_w, shared_down_w):
        import jax, jax.numpy as jnp
        import numpy as np
        B, S, H = (2, 256, 512)
        E, I = (64, 256)
        K = 8
        G, TG = (8, 4)
        SCALE = 2.5
        T = B * S
        CAP = 256

        def _moe_forward(x, router_w, gate_w, up_w, down_w, shared_gate_w, shared_up_w, shared_down_w):
            b, s, h = x.shape
            tokens = x.reshape(-1, h)
            t = tokens.shape[0]
            logits = tokens @ router_w
            scores = jax.nn.sigmoid(logits)
            eg = E // G
            group_scores = scores.reshape(t, G, eg).max(axis=-1)
            _, sel_groups = jax.lax.top_k(group_scores, TG)
            group_mask = jnp.zeros((t, G), bool).at[jnp.arange(t)[:, None], sel_groups].set(True)
            expert_mask = jnp.repeat(group_mask, eg, axis=1)
            masked_scores = jnp.where(expert_mask, scores, 0.0)
            topk_w, topk_idx = jax.lax.top_k(masked_scores, K)
            topk_w = topk_w / jnp.clip(topk_w.sum(-1, keepdims=True), 1e-09)
            topk_w = topk_w * SCALE
            flat_e = topk_idx.reshape(-1)
            onehot = jax.nn.one_hot(flat_e, E, dtype=jnp.int32)
            prior = jnp.cumsum(onehot, axis=0) - onehot
            pos = jnp.take_along_axis(prior, flat_e[:, None], axis=1)[:, 0]
            valid = (pos < CAP).astype(tokens.dtype)
            pos_c = jnp.minimum(pos, CAP - 1)
            tidx = jnp.repeat(jnp.arange(t), K)
            dispatch = jnp.zeros((E, CAP, h), tokens.dtype)
            dispatch = dispatch.at[flat_e, pos_c].add(tokens[tidx] * valid[:, None])
            g = jnp.einsum('ech,ehi->eci', dispatch, gate_w)
            u = jnp.einsum('ech,ehi->eci', dispatch, up_w)
            expert_out = jnp.einsum('eci,eih->ech', jax.nn.silu(g) * u, down_w)
            gathered = expert_out[flat_e, pos_c]
            contrib = gathered * (topk_w.reshape(-1) * valid)[:, None]
            output = jnp.zeros((t, h), tokens.dtype).at[tidx].add(contrib)
            sg = jax.nn.silu(tokens @ shared_gate_w) * (tokens @ shared_up_w)
            output = output + sg @ shared_down_w
            return output.reshape(b, s, h)
        return _moe_forward(x, router_w, gate_w, up_w, down_w, shared_gate_w, shared_up_w, shared_down_w)
    x = L0_attn_x
    xn = _layernorm(x, axis=-1)
    x = x + _L0_attn_ref(xn, L0_attn_input_weights, L0_attn_xis, L0_attn_proj_matrix) + _L0_ffn_ref(xn, L0_ffn_router_w, L0_ffn_gate_w, L0_ffn_up_w, L0_ffn_down_w, L0_ffn_shared_gate_w, L0_ffn_shared_up_w, L0_ffn_shared_down_w)
    return x

_drawn_inputs = setup_inputs


def setup_inputs(seed=0):
    import zlib

    import numpy as np

    out = dict(_drawn_inputs(seed))
    spreads = {}
    factors = {'L0_ffn_router_w': 2.97,
     'L0_ffn_gate_w': 2.981,
     'L0_ffn_up_w': 2.79,
     'L0_ffn_down_w': 2.794}
    for name, (base, spread) in spreads.items():
        noise = np.random.default_rng([zlib.crc32(name.encode()), seed]).standard_normal(out[name].shape)
        drawn = base * np.exp(spread * noise) if base else spread * noise
        out[name] = jnp.asarray(drawn.astype(out[name].dtype))
    for name, factor in factors.items():
        out[name] = (out[name] * factor).astype(out[name].dtype)
    return out
```

```python
from contextlib import ExitStack

import concourse.bass as bass
from concourse import mybir

ALU = mybir.AluOpType
ACT = mybir.ActivationFunctionType
F32 = mybir.dt.float32
F32R = mybir.dt.float32r
BF16 = mybir.dt.bfloat16
I32 = mybir.dt.int32
U32 = mybir.dt.uint32
AX_X = mybir.AxisListType.X

P = 128
H = 512
HB = H // P
TOKENS = 8192
GROUP = 512
J = GROUP // P
GROUPS = TOKENS // GROUP
E = 64
EG = 8
RG = E // EG
TOP_GROUPS = 4
K = 8
CAP = 256
CB = CAP // P
I = 256
IB = I // P
SCALE = 2.5
EPS = 1e-5
RSQRT_SEED = 0x5F3759DF
SLOTS = E * CAP
SPARE = CAP
ROW = H + E
GU = 2 * HB * I
DN = IB * H
OUTSIDE = 2 * SLOTS
SCATTER = 16 * J * K


class Turn:

    def __init__(self, i, b):
        self.i, self.b = i, b
        self.n = 2 * i + b

    def next(self):
        return Turn(self.i, 1) if self.b == 0 else Turn(self.i + 1, 0)

    def prev(self):
        return Turn(self.i, 0) if self.b == 1 else Turn(self.i - 1, 1)


def turn(n):
    return Turn(n // 2, n % 2)


def at_least(eng, sem, value):
    if not (isinstance(value, int) and value <= 0):
        eng.wait_ge(sem, value)


def build(nc, x, iw, xis, proj, router_w, gate_w, up_w, down_w, sgate_w, sup_w, sdown_w, out):
    with ExitStack() as ctx:
        def sb(name, shape, dt=F32):
            return ctx.enter_context(nc.sbuf_tensor(name, shape, dt))

        def ps(name, shape):
            return ctx.enter_context(nc.psum_tensor(name, shape, F32))

        def sem(name):
            return ctx.enter_context(nc.semaphore(name))

        rows = nc.dram_tensor("rows", [TOKENS + SPARE, ROW], F32).ap()
        slot_token = nc.dram_tensor("slot_token", [SLOTS, 1], F32).ap()

        ident = sb("ident", [P, P])
        before = sb("before", [P, P], BF16)
        ones = sb("ones", [P, P], BF16)
        lower = sb("lower", [P, RG, RG])
        expert_base = sb("expert_base", [P, E])
        token_ids_i = sb("token_ids_i", [P, GROUPS * J], I32)
        token_ids = sb("token_ids", [P, GROUPS * J])
        expert_base_i = sb("expert_base_i", [P, E], I32)
        proj_hi = sb("proj_hi", [P, HB, H], F32R)
        proj_lo = sb("proj_lo", [P, HB, H], F32R)
        wt_hi = sb("wt_hi", [P, HB, H], F32R)
        wt_lo = sb("wt_lo", [P, HB, H], F32R)
        sgu_hi = sb("sgu_hi", [P, GU], F32R)
        sgu_lo = sb("sgu_lo", [P, GU], F32R)
        sdn_hi = sb("sdn_hi", [P, DN], F32R)
        sdn_lo = sb("sdn_lo", [P, DN], F32R)
        router = sb("router", [P, HB, 2 * E], F32R)
        xis_row = sb("xis_row", [HB, P])
        ab = sb("ab", [P, HB])
        ab2 = sb("ab2", [P, HB])
        corr = sb("corr", [P, HB])
        corr_r = sb("corr_r", [P, HB], F32R)
        corr3 = sb("corr3", [P, HB, 3])
        corr_row = sb("corr_row", [3, H], F32R)
        xbuf = [sb(f"xbuf{b}", [P, J, H]) for b in range(2)]
        xn = sb("xn", [P, J, H])
        xt_hi = [sb(f"xt_hi{b}", [P, HB, GROUP], F32R) for b in range(2)]
        xt_lo = [sb(f"xt_lo{b}", [P, HB, GROUP], F32R) for b in range(2)]
        wait_carrier = sb("wait_carrier", [P, 1])
        pool_carrier = sb("pool_carrier", [P, 1])
        pool_sink = sb("pool_sink", [P, 1])
        stats = sb("stats", [P, J, 6])
        mean_var = sb("mean_var", [P, J, 2])
        var_eps = sb("var_eps", [P, J])
        rstd = sb("rstd", [P, J])
        rstd2 = sb("rstd2", [P, J])
        norm = sb("norm", [P, J])
        norm_r = sb("norm_r", [P, J], F32R)
        norm3 = sb("norm3", [P, J, 3])
        norm_row = [sb(f"norm_row{b}", [3, GROUP], F32R) for b in range(2)]
        feat = sb("feat", [P, 2, GROUP])
        feat_hi = sb("feat_hi", [P, HB, GROUP], F32R)
        feat_lo = sb("feat_lo", [P, HB, GROUP], F32R)
        gate_t = sb("gate_t", [P, GROUP])
        gate_a = sb("gate_a", [P, GROUP])
        hid = sb("hid", [P, GROUP])
        hid_hi = sb("hid_hi", [P, 2, IB, CAP], F32R)
        hid_lo = sb("hid_lo", [P, 2, IB, CAP], F32R)
        shid_hi = hid_hi[:].rearrange("p a b c -> p (a b c)").rearrange("p (i t) -> p i t", i=IB)
        shid_lo = hid_lo[:].rearrange("p a b c -> p (a b c)").rearrange("p (i t) -> p i t", i=IB)
        outs = [sb(f"outs{b}", [P, 2, H]) for b in range(2)]
        router_raw = gate_a[:, 0:HB * E].rearrange("p (c e) -> p c e", c=HB)
        square = hid
        zeros = outs[0][:].rearrange("p a h -> p (a h)")[:, 0:ROW]
        no_token_i = outs[1][0:E, 0, 0:CAP].bitcast(I32)
        no_token = outs[1][0:E, 1, 0:CAP]
        logit = sb("logit", [P, J, E])
        expn = sb("expn", [P, J, E])
        score = sb("score", [P, J, E])
        gmax = sb("gmax", [P, J, RG])
        beats = sb("beats", [P, J, RG, 2 * RG])
        rank = sb("rank", [P, J * RG])
        masked = sb("masked", [P, J, E])
        top = sb("top", [P, J, K])
        taken = sb("taken", [P, J, E])
        chosen = sb("chosen", [P, J, E], BF16)
        wsum = sb("wsum", [P, J])
        weight = sb("weight", [P, J, E])
        nchosen = sb("nchosen", [P, E])
        earlier = [sb(f"earlier{b}", [P, E], BF16) for b in range(2)]
        key = sb("key", [P, J, E])
        key8 = sb("key8", [P, J, K])
        slots = [sb(f"slots{b}", [P, J, K], U32) for b in range(2)]
        ids = [sb(f"ids{b}", [P, J]) for b in range(2)]
        raw = [sb(f"raw{b}", [P, GU + DN]) for b in range(2)]
        slot_rows = key[:].rearrange("p j e -> p (j e)")[:, 0:P]
        slot_cols = sb("slot_cols", [P, P], U32)
        gidx = [sb(f"gidx{b}", [P, CB], U32) for b in range(2)]
        sidx = [sb(f"sidx{b}", [P, CB], U32) for b in range(2)]
        slot_w = [sb(f"slot_w{b}", [P, CB]) for b in range(2)]
        xe = [xbuf[b][:].rearrange("p j h -> p (j h)")[:, 0:CB * ROW].rearrange("p (c h) -> p c h", c=CB)
              for b in range(2)]
        egu_hi = [proj_hi[:].rearrange("p a b -> p (a b)"), sgu_hi[:, :]]
        egu_lo = [proj_lo[:].rearrange("p a b -> p (a b)"), sgu_lo[:, :]]
        edn_hi = [sdn_hi[:, :], feat_hi[:, 0:IB, :].rearrange("p a b -> p (a b)")]
        edn_lo = [sdn_lo[:, :], feat_lo[:, 0:IB, :].rearrange("p a b -> p (a b)")]

        ptr = ps("ptr", [P, 2, 512])
        pmm = [ps(f"pmm{b}", [P, 512]) for b in range(2)]
        pout = [ps(f"pout{b}", [P, 512]) for b in range(2)]
        plog = ps("plog", [P, 512])
        ppos = ps("ppos", [P, 512])
        ptr_e = ptr[:].rearrange("p a b -> p (a b)").rearrange("p (h c) -> p h c", h=HB)

        consts_made = sem("consts_made")
        pool_step = sem("pool_step")
        xis_loaded = sem("xis_loaded")
        proj_loaded = sem("proj_loaded")
        iw_loaded = sem("iw_loaded")
        router_loaded = sem("router_loaded")
        table_made = sem("table_made")
        xis_turned = sem("xis_turned")
        proj_scaled = sem("proj_scaled")
        corr3_made = sem("corr3_made")
        corr_turned = sem("corr_turned")
        corr_row_made = sem("corr_row_made")
        ab2_exp = sem("ab2_exp")
        ab2_made = sem("ab2_made")
        router_hi_made = sem("router_hi_made")
        router_made = sem("router_made")
        shared_hi_made = sem("shared_hi_made")
        shared_lo_made = sem("shared_lo_made")
        vec_step = sem("vec_step")
        x_loaded = [sem(f"x_loaded{b}") for b in range(2)]
        xn_made = sem("xn_made")
        norm3_made = sem("norm3_made")
        xn_stored = sem("xn_stored")
        w_made = sem("w_made")
        w_stored = sem("w_stored")
        turned = sem("turned")
        xt_hi_made = sem("xt_hi_made")
        xt_lo_made = sem("xt_lo_made")
        norm_row_made = sem("norm_row_made")
        dot_done = sem("dot_done")
        exp_done = sem("exp_done")
        feat_hi_made = sem("feat_hi_made")
        feat_lo_made = sem("feat_lo_made")
        gate_done = sem("gate_done")
        up_done = sem("up_done")
        tanh_done = sem("tanh_done")
        hid_made = sem("hid_made")
        hid_hi_made = sem("hid_hi_made")
        hid_lo_made = sem("hid_lo_made")
        out_done = sem("out_done")
        out_free = sem("out_free")
        out_stored = [sem(f"out_stored{b}") for b in range(2)]
        logits_done = sem("logits_done")
        logit_made = sem("logit_made")
        expn_made = sem("expn_made")
        chosen_made = sem("chosen_made")
        pos_done = sem("pos_done")
        slots_made = sem("slots_made")
        scattered = [sem(f"scattered{b}") for b in range(2)]
        slot_rows_loaded = sem("slot_rows_loaded")
        slot_rows_turned = sem("slot_rows_turned")
        slot_cols_made = sem("slot_cols_made")
        gu_loaded = [sem(f"gu_loaded{b}") for b in range(2)]
        dn_loaded = [sem(f"dn_loaded{b}") for b in range(2)]
        idx_copied = sem("idx_copied")
        gathered = [sem(f"gathered{b}") for b in range(2)]
        slot_w_made = sem("slot_w_made")
        e_turned = sem("e_turned")
        e_xt_hi_made = sem("e_xt_hi_made")
        e_xt_lo_made = sem("e_xt_lo_made")
        egu_hi_made = sem("egu_hi_made")
        egu_lo_made = sem("egu_lo_made")
        edn_hi_made = sem("edn_hi_made")
        edn_lo_made = sem("edn_lo_made")
        e_gate_done = sem("e_gate_done")
        e_up_done = sem("e_up_done")
        silu_done = sem("silu_done")
        e_hid_made = sem("e_hid_made")
        e_hid_hi_made = sem("e_hid_hi_made")
        e_hid_lo_made = sem("e_hid_lo_made")
        down_done = sem("down_done")
        e_out_made = sem("e_out_made")
        added = sem("added")

        x_groups = x.rearrange("b s h -> (b s) h").rearrange("(g j p) h -> g p j h", j=J, p=P)
        rows_groups = rows[0:TOKENS, :].rearrange("(g j p) h -> g p j h", j=J, p=P)
        out_halves = out[0:TOKENS, :].rearrange("(g a j p) h -> g a p j h", a=2, j=2, p=P)

        block = ctx.enter_context(nc.Block())

        @block.sync
        def _(sp):
            def load_x(g):
                sp.dma_start(xbuf[g.b][:], x_groups[g.n]).then_inc(x_loaded[g.b], 16)

            def load_gate_up(b, gate, up):
                sp.dma_start(raw[b][:, 0:GU // 2].rearrange("p (c i) -> p c i", c=HB),
                             gate.rearrange("(c p) i -> p c i", p=P)).then_inc(gu_loaded[b], 16)
                sp.dma_start(raw[b][:, GU // 2:GU].rearrange("p (c i) -> p c i", c=HB),
                             up.rearrange("(c p) i -> p c i", p=P)).then_inc(gu_loaded[b], 16)

            def load_down(b, down):
                sp.dma_start(raw[b][:, GU:].rearrange("p (c h) -> p c h", c=IB),
                             down.rearrange("(c p) h -> p c h", p=P)).then_inc(dn_loaded[b], 16)

            def store_xn(g):
                sp.wait_ge(xn_made, g.n + 1)
                sp.dma_start(rows_groups[g.n][:, :, 0:H], xn[:]).then_inc(xn_stored, 16)

            def store_w(g):
                sp.wait_ge(w_made, g.n + 1)
                sp.dma_start(rows_groups[g.n][:, :, H:ROW], weight[:]).then_inc(w_stored, 16)

            def store_out(g):
                for a in range(2):
                    sp.wait_ge(out_free, 2 + J * g.n + 2 * a + 2)
                    sp.dma_start(out_halves[g.n, a], outs[a][:]).then_inc(out_stored[a], 16)

            def group(g, last=False):
                if not last:
                    store_xn(g.next())
                    store_w(g.next())
                store_out(g)

            sp.dma_start(xis_row[:], xis.rearrange("(c p) -> c p", p=P)).then_inc(xis_loaded, 16)
            sp.dma_start(xbuf[1][:], proj.rearrange("(c p) d -> p c d", p=P)).then_inc(proj_loaded, 16)
            sp.dma_start(xn[:], iw.rearrange("(c p) d -> p c d", p=P)).then_inc(iw_loaded, 16)
            load_x(turn(0))
            sp.dma_start(router_raw, router_w.rearrange("(c p) e -> p c e", p=P)).then_inc(router_loaded, 16)
            load_gate_up(0, sgate_w, sup_w)
            load_down(0, sdown_w)
            load_gate_up(1, gate_w[1], up_w[1])
            load_down(1, down_w[1])
            sp.wait_ge(consts_made, 1)
            sp.dma_start(slot_token.rearrange("(e s) o -> e (s o)", s=CAP), no_token).then_inc(table_made, 16)
            for c in range(SPARE // P):
                at = slice(TOKENS + c * P, TOKENS + (c + 1) * P)
                sp.dma_start(rows[at, :], zeros).then_inc(table_made, 16)
                sp.dma_start(out[at, :], zeros[:, 0:H]).then_inc(table_made, 16)
            sp.wait_ge(turned, 2)
            load_x(turn(1))
            store_xn(turn(0))
            sp.wait_ge(shared_lo_made, 2)
            load_gate_up(0, gate_w[0], up_w[0])
            load_down(0, down_w[0])
            store_w(turn(0))
            with sp.Fori(0, GROUPS // 2 - 1) as i:
                for b in range(2):
                    g = Turn(i, b)
                    group(g)
                    sp.wait_ge(out_free, 2 + J * g.n + J)
                    load_x(Turn(i + 1, b))
            group(turn(GROUPS - 2))
            for b in range(2):
                sp.wait_ge(scattered[b], SCATTER * GROUPS // 2)
            sp.dma_start(slot_rows, slot_token.rearrange("(q p) o -> q (p o)", p=P)).then_inc(
                slot_rows_loaded, 16)
            group(turn(GROUPS - 1), last=True)

            def refill(e):
                b = e.b
                sp.wait_ge(egu_hi_made, e.n - 1)
                sp.wait_ge(egu_lo_made, e.n - 1)
                load_gate_up(b, gate_w[e.n], up_w[e.n])
                sp.wait_ge(edn_hi_made, e.n - 1)
                sp.wait_ge(edn_lo_made, e.n - 1)
                load_down(b, down_w[e.n])

            with sp.Fori(1, E // 2) as i:
                for b in range(2):
                    refill(Turn(i, b))

        @block.scalar
        def _(act):
            copy = ACT.Copy

            def hi_block(n, b, dst):
                for half in range(2):
                    act.wait_ge(turned, 2 * n + half + 1)
                    act.activation(dst[:, 2 * half:2 * half + 2, :], ptr[:], copy).then_inc(xt_hi_made, 1)
                    if half == 1 and b is not None:
                        act.activation(norm_row[b][:], ppos[0:3, :], copy).then_inc(norm_row_made, 1)

            def features(s, r, hi, scale=None):
                act.wait_ge(dot_done, HB * s + r + 1)
                at_least(act, feat_lo_made, HB * s + r - 1)
                act.activation(feat[:, r % 2], pmm[r % 2][:], ACT.Exp).then_inc(exp_done, 1)
                act.wait_ge(exp_done, HB * s + r + 1)
                if scale is None:
                    act.activation(hi[:, r, :], feat[:, r % 2], copy).then_inc(feat_hi_made, 1)
                else:
                    act.activation(hi[:, r, :], feat[:, r % 2], copy, scale=scale).then_inc(feat_hi_made, 1)

            def hidden(g, i):
                act.wait_ge(gate_done, IB * g.n + i + 1)
                at_least(act, hid_made, IB * g.n + i)
                act.activation(gate_t[:], pmm[0][:], ACT.Tanh, scale=0.5).then_inc(tanh_done, 1)

            def hidden_hi(g, i):
                act.wait_ge(hid_made, IB * g.n + i + 1)
                act.activation(shid_hi[:, i, :], hid[:], copy).then_inc(hid_hi_made, 1)

            def exp_logits(g):
                act.wait_ge(logit_made, g.n + 1)
                act.activation(expn[:], logit[:], ACT.Exp, scale=-1.0).then_inc(expn_made, 1)

            def hi_half(g, half):
                act.wait_ge(turned, 2 * (g.n + 2) + half + 1)
                act.activation(xt_hi[g.b][:, 2 * half:2 * half + 2, :], ptr[:], copy).then_inc(xt_hi_made, 1)

            def hi_norm(g):
                act.activation(norm_row[g.b][:], ppos[0:3, :], copy).then_inc(norm_row_made, 1)

            def group(g, last=False):
                for r in range(HB):
                    features(1 + g.n, r, feat_hi)
                if not last:
                    hi_half(g.next(), 0)
                hidden(g, 0)
                hidden_hi(g, 0)
                if not last:
                    hi_half(g.next(), 1)
                    hi_norm(g.next())
                hidden(g, 1)
                hidden_hi(g, 1)
                if not last:
                    exp_logits(g.next())

            act.wait_ge(vec_step, 1)
            act.activation(ab2[:], ab[:], ACT.Exp, scale=2.0).then_inc(ab2_exp, 1)
            act.wait_ge(router_loaded, 16)
            act.activation(router[:, :, 0:E], router_raw, copy).then_inc(router_hi_made, 1)
            act.wait_ge(corr_turned, 1)
            act.activation(corr_row[:], ppos[0:3, :], copy).then_inc(corr_row_made, 1)
            hi_block(0, None, proj_hi)
            hi_block(1, 1, xt_hi[1])
            act.wait_ge(ab2_made, 1)
            for r in range(HB):
                features(0, r, wt_hi, scale=ab2[:, r:r + 1])
            act.wait_ge(gu_loaded[0], 32)
            act.activation(sgu_hi[:], raw[0][:, 0:GU], copy).then_inc(shared_hi_made, 1)
            act.wait_ge(dn_loaded[0], 16)
            act.activation(sdn_hi[:], raw[0][:, GU:], copy).then_inc(shared_hi_made, 1)
            hi_half(turn(0), 0)
            hi_half(turn(0), 1)
            hi_norm(turn(0))
            exp_logits(turn(0))
            group(turn(0))
            group(turn(1))
            with act.Fori(1, GROUPS // 2 - 1) as i:
                for b in range(2):
                    group(Turn(i, b))
            group(turn(GROUPS - 2))
            group(turn(GROUPS - 1), last=True)

            def gate_up_hi(e, at_start=False):
                if at_start:
                    act.wait_ge(dot_done, HB * (GROUPS + 1))
                act.wait_ge(gu_loaded[e.b], 32 * (e.i + (2 if e.b == 0 else 1)))
                act.activation(egu_hi[e.b], raw[e.b][:, 0:GU], copy).then_inc(egu_hi_made, 1)

            def down_hi(e):
                act.wait_ge(dn_loaded[e.b], 16 * (e.i + (2 if e.b == 0 else 1)))
                act.activation(edn_hi[e.b], raw[e.b][:, GU:], copy).then_inc(edn_hi_made, 1)

            def e_turned_hi(e):
                act.wait_ge(e_turned, e.n + 1)
                act.activation(xt_hi[e.b][:, :, 0:CAP], ptr_e, copy).then_inc(e_xt_hi_made, 1)

            def e_silu(e):
                act.wait_ge(e_gate_done, e.n + 1)
                at_least(act, e_hid_made, e.n)
                act.activation(gate_t[:], pmm[0][:], ACT.Silu).then_inc(silu_done, 1)

            def e_hidden_hi(e):
                act.wait_ge(e_hid_made, e.n + 1)
                act.activation(hid_hi[:, e.b].rearrange("p a b -> p (a b)"), hid[:], copy).then_inc(
                    e_hid_hi_made, 1)

            def e_out(e):
                act.wait_ge(slot_w_made, e.n + 1)
                at_least(act, added, 16 * CB * (e.n - 1))
                for c in range(CB):
                    act.wait_ge(down_done, CB * e.n + c + 1)
                    act.activation(outs[e.b][:, c], pout[c][:], copy, scale=slot_w[e.b][:, c:c + 1]).then_inc(
                        e_out_made, 1)

            def stage(e, turn_next=True, run=True, out_prev=True):
                if turn_next:
                    e_turned_hi(e.next())
                    gate_up_hi(e.next())
                if run:
                    e_silu(e)
                    down_hi(e)
                    e_hidden_hi(e)
                if out_prev:
                    e_out(e.prev())

            gate_up_hi(turn(0), at_start=True)
            e_turned_hi(turn(0))
            for b in range(2):
                act.wait_ge(out_stored[b], 16 * GROUPS)
            stage(turn(0), out_prev=False)
            stage(turn(1))
            with act.Fori(1, E // 2 - 1) as i:
                for b in range(2):
                    stage(Turn(i, b))
            stage(turn(E - 2))
            stage(turn(E - 1), turn_next=False)
            e_out(turn(E - 1))

        @block.vector
        def _(dve):
            steps = [0]

            def step(ins, base=0, apart=False):
                ins.then_inc(vec_step, 1)
                steps[0] += 1
                dve.wait_ge(vec_step, base + steps[0])
                if apart:
                    dve.memset(wait_carrier[:], 0.0)

            def split_norm(base=0):
                step(dve.tensor_copy(norm_r[:], norm[:]), base)
                dve.tensor_copy(norm3[:, :, 0:2], norm_r[:].bitcast(F32).unsqueeze(2).to_broadcast([P, J, 2]))
                dve.tensor_tensor(norm3[:, :, 2], norm[:], norm_r[:].bitcast(F32), ALU.subtract).then_inc(
                    norm3_made, 1)

            def lo_half(n, half, hi, lo):
                dve.wait_ge(xt_hi_made, 2 * n + half + 1)
                at = slice(2 * half, 2 * half + 2)
                dve.tensor_tensor(lo[:, at, :], ptr[:], hi[:, at, :].bitcast(F32), ALU.subtract).then_inc(
                    xt_lo_made, 1)

            def features_lo(s, r, hi, lo, scale=1.0):
                dve.wait_ge(feat_hi_made, HB * s + r + 1)
                if isinstance(scale, float):
                    ins = dve.tensor_tensor(lo[:, r, :], feat[:, r % 2], hi[:, r, :].bitcast(F32), ALU.subtract)
                else:
                    ins = dve.scalar_tensor_tensor(out=lo[:, r, :], in0=feat[:, r % 2], scalar=scale,
                                                   in1=hi[:, r, :].bitcast(F32), op0=ALU.mult,
                                                   op1=ALU.subtract)
                ins.then_inc(feat_lo_made, 1)

            def normalise(g, base):
                dve.wait_ge(x_loaded[g.b], 16 * (g.i + 1))
                for j in range(J):
                    ins = dve.bn_stats(stats[:, j, :], xbuf[g.b][:, j, :])
                step(ins, base, apart=True)
                for j in range(J):
                    ins = dve.bn_aggr(mean_var[:, j, :], stats[:, j, :])
                step(ins, base)
                step(dve.tensor_scalar(var_eps[:], mean_var[:, :, 1], EPS, None, ALU.add), base)
                step(dve.tensor_scalar(rstd2[:].bitcast(I32), var_eps[:].bitcast(I32), 1, None,
                                       ALU.arith_shift_right), base)
                step(dve.tensor_scalar(rstd[:].bitcast(I32), rstd2[:].bitcast(I32), -1.0,
                                       float(RSQRT_SEED), ALU.mult, ALU.add), base)
                for _ in range(3):
                    step(dve.tensor_tensor(rstd2[:], rstd[:], rstd[:], ALU.mult), base)
                    step(dve.scalar_tensor_tensor(out=rstd2[:], in0=rstd2[:], scalar=-0.5, in1=var_eps[:],
                                                  op0=ALU.mult, op1=ALU.mult), base)
                    step(dve.scalar_tensor_tensor(out=rstd[:], in0=rstd2[:], scalar=1.5, in1=rstd[:],
                                                  op0=ALU.add, op1=ALU.mult), base)
                dve.wait_ge(turned, 2 * (g.n + 2))
                at_least(dve, xn_stored, 16 * g.n)
                for j in range(J):
                    ins = dve.tensor_scalar(xn[:, j, :], xbuf[g.b][:, j, :], mean_var[:, j, 0:1],
                                            rstd[:, j:j + 1], ALU.subtract, ALU.mult)
                ins.then_inc(xn_made, 1)
                step(dve.tensor_tensor(rstd2[:], rstd[:], rstd[:], ALU.mult), base)
                step(dve.scalar_tensor_tensor(out=norm[:], in0=mean_var[:, :, 1], scalar=float(H),
                                              in1=rstd2[:], op0=ALU.mult, op1=ALU.mult), base)
                split_norm(base)

            def choose(g, base):
                lg = plog[:].rearrange("p (j a e) -> p j a e", j=J, a=2)
                dve.wait_ge(logits_done, g.n + 1)
                step(dve.tensor_copy(logit[:], lg[:, :, 0, :]), base)
                dve.tensor_tensor(logit[:], logit[:], lg[:, :, 1, :], ALU.add).then_inc(logit_made, 1)
                dve.wait_ge(expn_made, g.n + 1)
                step(dve.tensor_scalar(expn[:], expn[:], 1.0, None, ALU.add), base)
                step(dve.reciprocal(score[:], expn[:]), base)
                step(dve.tensor_reduce(gmax[:], score[:].rearrange("p j (g e) -> p (j g) e", e=EG), AX_X,
                                       ALU.max), base)
                other = gmax[:].unsqueeze(2).to_broadcast([P, J, RG, RG])
                own = gmax[:].unsqueeze(3).to_broadcast([P, J, RG, RG])
                dve.tensor_tensor(beats[:, :, :, 0:RG], other, own, ALU.is_gt)
                step(dve.tensor_tensor(beats[:, :, :, RG:], other, own, ALU.is_equal), base)
                step(dve.tensor_tensor(beats[:, :, :, RG:], beats[:, :, :, RG:],
                                       lower[:].unsqueeze(1).to_broadcast([P, J, RG, RG]), ALU.mult), base)
                step(dve.tensor_reduce(rank[:], beats[:].rearrange("p j g o -> p (j g) o"), AX_X, ALU.add), base)
                step(dve.scalar_tensor_tensor(
                    out=masked[:].rearrange("p j (g e) -> p (j g) e", e=EG),
                    in0=rank[:].unsqueeze(2).to_broadcast([P, J * RG, EG]), scalar=float(TOP_GROUPS),
                    in1=score[:].rearrange("p j (g e) -> p (j g) e", e=EG), op0=ALU.is_lt, op1=ALU.mult), base,
                    apart=True)
                for j in range(J):
                    ins = dve.max(top[:, j, :], masked[:, j, :])
                step(ins, base, apart=True)
                for j in range(J):
                    ins = dve.match_replace(taken[:, j, :], top[:, j, :], masked[:, j, :], -1.0)
                step(ins, base)
                dve.tensor_scalar(chosen[:], taken[:], 0.0, None, ALU.is_lt).then_inc(chosen_made, 1)
                step(dve.tensor_reduce(wsum[:], top[:], AX_X, ALU.add), base)
                step(dve.tensor_scalar(wsum[:], wsum[:], 1e-9, None, ALU.max), base)
                step(dve.reciprocal(wsum[:], wsum[:]), base)
                at_least(dve, w_stored, 16 * g.n)
                step(dve.scalar_tensor_tensor(out=weight[:], in0=taken[:], scalar=0.0, in1=masked[:],
                                              op0=ALU.is_lt, op1=ALU.mult), base)
                dve.scalar_tensor_tensor(out=weight[:], in0=weight[:], scalar=SCALE,
                                         in1=wsum[:].unsqueeze(2).to_broadcast([P, J, E]),
                                         op0=ALU.mult, op1=ALU.mult).then_inc(w_made, 1)
                step(dve.tensor_reduce(nchosen[:], chosen[:].rearrange("p j e -> p e j"), AX_X, ALU.add), base)

            def place(g, base):
                pos = ppos[:, 0:J * E].rearrange("p (j e) -> p j e", j=J)
                dve.wait_ge(pos_done, g.n + 1)
                dve.tensor_tensor(earlier[1 - g.b][:], earlier[g.b][:], nchosen[:], ALU.add)
                dve.scalar_tensor_tensor(out=masked[:], in0=pos, scalar=float(CAP), in1=chosen[:],
                                         op0=ALU.is_lt, op1=ALU.mult)
                step(dve.tensor_tensor(key[:], expert_base[:].unsqueeze(1).to_broadcast([P, J, E]), pos,
                                       ALU.subtract), base)
                step(dve.tensor_tensor(key[:], key[:], masked[:], ALU.mult), base, apart=True)
                for j in range(J):
                    ins = dve.max(key8[:, j, :], key[:, j, :])
                step(ins, base)
                at_least(dve, scattered[g.b], SCATTER * g.i)
                dve.tensor_scalar(slots[g.b][:], key8[:], -1.0, float(OUTSIDE), ALU.mult, ALU.add).then_inc(
                    slots_made, 1)

            def hidden(g, i, base):
                dve.wait_ge(tanh_done, IB * g.n + i + 1)
                step(dve.scalar_tensor_tensor(out=gate_a[:], in0=gate_t[:], scalar=1.0, in1=pmm[0][:],
                                              op0=ALU.add, op1=ALU.mult), base)
                dve.wait_ge(up_done, IB * g.n + i + 1)
                at_least(dve, hid_hi_made, IB * g.n + i)
                dve.scalar_tensor_tensor(out=hid[:], in0=gate_a[:], scalar=0.5, in1=pmm[1][:],
                                         op0=ALU.mult, op1=ALU.mult).then_inc(hid_made, 1)

            def hidden_lo(g, i):
                dve.wait_ge(hid_hi_made, IB * g.n + i + 1)
                dve.tensor_tensor(shid_lo[:, i, :], hid[:], shid_hi[:, i, :].bitcast(F32),
                                  ALU.subtract).then_inc(hid_lo_made, 1)

            def output(g, j):
                dve.wait_ge(out_done, J * g.n + j + 1)
                if j % 2 == 0:
                    at_least(dve, out_stored[j // 2], 16 * g.n)
                dve.tensor_tensor(outs[j // 2][:, j % 2, :], pout[j % 2][:], xbuf[g.b][:, j, :],
                                  ALU.add).then_inc(out_free, 1)

            def group(g, base, last=False):
                nxt = g.next()
                features_lo(1 + g.n, 0, feat_hi, feat_lo)
                if not last:
                    normalise(nxt, base)
                for r in range(1, HB):
                    features_lo(1 + g.n, r, feat_hi, feat_lo)
                if not last:
                    lo_half(nxt.n + 2, 0, xt_hi[nxt.b], xt_lo[nxt.b])
                hidden(g, 0, base)
                hidden_lo(g, 0)
                if not last:
                    lo_half(nxt.n + 2, 1, xt_hi[nxt.b], xt_lo[nxt.b])
                hidden(g, 1, base)
                hidden_lo(g, 1)
                if last:
                    gate_up_lo(turn(0))
                else:
                    choose(nxt, base)
                output(g, 0)
                output(g, 1)
                if last:
                    dve.wait_ge(slot_rows_turned, 1)
                    dve.tensor_copy(slot_cols[:], plog[:, 0:P]).then_inc(slot_cols_made, 1)
                else:
                    place(nxt, base)
                output(g, 2)
                output(g, 3)

            def gate_up_lo(e):
                dve.wait_ge(egu_hi_made, e.n + 1)
                dve.tensor_tensor(egu_lo[e.b], raw[e.b][:, 0:GU], egu_hi[e.b].bitcast(F32),
                                  ALU.subtract).then_inc(egu_lo_made, 1)

            dve.memset(earlier[0][:], 0.0).then_inc(out_free, 2)
            dve.wait_ge(xis_turned, 1)
            step(dve.tensor_copy(ab[:], ppos[:, 0:HB]))
            dve.wait_ge(proj_loaded, 16)
            for r in range(HB):
                ins = dve.tensor_scalar(xbuf[1][:, r, :], xbuf[1][:, r, :], ab[:, r:r + 1], None, ALU.mult)
            ins.then_inc(proj_scaled, 1)
            step(dve.scalar_tensor_tensor(out=corr[:], in0=ab[:], scalar=-0.5, in1=ab[:], op0=ALU.mult,
                                          op1=ALU.mult))
            step(dve.tensor_copy(corr_r[:], corr[:]))
            dve.tensor_copy(corr3[:, :, 0], corr_r[:].bitcast(F32))
            dve.tensor_copy(corr3[:, :, 2], corr_r[:].bitcast(F32))
            dve.tensor_tensor(corr3[:, :, 1], corr[:], corr_r[:].bitcast(F32), ALU.subtract).then_inc(
                corr3_made, 1)
            dve.wait_ge(ab2_exp, 1)
            dve.tensor_scalar(ab2[:], ab2[:], 1.0 / H, None, ALU.mult).then_inc(ab2_made, 1)
            dve.wait_ge(iw_loaded, 16)
            for r in range(HB):
                step(dve.tensor_tensor_reduce(out=square[:], in0=xn[:, r, :], in1=xn[:, r, :], scale=1.0,
                                              scalar=0.0, op0=ALU.mult, op1=ALU.add,
                                              accum_out=norm[:, r:r + 1]))
            split_norm()
            dve.wait_ge(router_hi_made, 1)
            dve.tensor_tensor(router[:, :, E:], router_raw, router[:, :, 0:E].bitcast(F32),
                              ALU.subtract).then_inc(router_made, 1)
            for half in range(2):
                lo_half(0, half, proj_hi, proj_lo)
            for half in range(2):
                lo_half(1, half, xt_hi[1], xt_lo[1])
            normalise(turn(0), 0)
            for r in range(HB):
                features_lo(0, r, wt_hi, wt_lo, scale=ab2[:, r:r + 1])
            dve.wait_ge(shared_hi_made, 1)
            dve.tensor_tensor(sgu_lo[:], raw[0][:, 0:GU], sgu_hi[:].bitcast(F32), ALU.subtract).then_inc(
                shared_lo_made, 1)
            dve.wait_ge(shared_hi_made, 2)
            dve.tensor_tensor(sdn_lo[:], raw[0][:, GU:], sdn_hi[:].bitcast(F32), ALU.subtract).then_inc(
                shared_lo_made, 1)
            for half in range(2):
                lo_half(2, half, xt_hi[0], xt_lo[0])
            dve.wait_ge(consts_made, 1)
            choose(turn(0), 0)
            place(turn(0), 0)

            dve.wait_ge(table_made, 16 * (1 + 2 * SPARE // P))
            start, per_group = steps[0], 37
            for n in range(2):
                steps[0] = 0
                group(turn(n), start + per_group * n)
            with dve.Fori(1, GROUPS // 2 - 1) as i:
                for b in range(2):
                    steps[0] = 0
                    group(Turn(i, b), start + per_group * (2 * i + b))
                    assert steps[0] == per_group, steps
            steps[0] = 0
            group(turn(GROUPS - 2), start + per_group * (GROUPS - 2))
            steps[0] = 0
            group(turn(GROUPS - 1), start + per_group * (GROUPS - 1), last=True)

            def down_lo(e):
                dve.wait_ge(edn_hi_made, e.n + 1)
                dve.tensor_tensor(edn_lo[e.b], raw[e.b][:, GU:], edn_hi[e.b].bitcast(F32),
                                  ALU.subtract).then_inc(edn_lo_made, 1)

            def e_turned_lo(e):
                dve.wait_ge(e_xt_hi_made, e.n + 1)
                dve.tensor_tensor(xt_lo[e.b][:, :, 0:CAP], ptr_e, xt_hi[e.b][:, :, 0:CAP].bitcast(F32),
                                  ALU.subtract).then_inc(e_xt_lo_made, 1)

            def slot_weights(e):
                at_least(dve, e_out_made, CB * (e.n - 1))
                dve.tensor_copy(slot_w[e.b][:].unsqueeze(2), xe[e.b][:, :, bass.ds(H + e.n, 1)]).then_inc(
                    slot_w_made, 1)

            def e_hidden(e):
                dve.wait_ge(silu_done, e.n + 1)
                dve.wait_ge(e_up_done, e.n + 1)
                at_least(dve, e_hid_hi_made, e.n)
                at_least(dve, e_hid_lo_made, e.n)
                dve.tensor_tensor(hid[:], gate_t[:], pmm[1][:], ALU.mult).then_inc(e_hid_made, 1)

            def e_hidden_lo(e):
                dve.wait_ge(e_hid_hi_made, e.n + 1)
                dve.tensor_tensor(hid_lo[:, e.b].rearrange("p a b -> p (a b)"), hid[:],
                                  hid_hi[:, e.b].rearrange("p a b -> p (a b)").bitcast(F32),
                                  ALU.subtract).then_inc(e_hid_lo_made, 1)

            def stage(e, turn_next=True):
                slot_weights(e)
                if turn_next:
                    e_turned_lo(e.next())
                    gate_up_lo(e.next())
                e_hidden(e)
                down_lo(e)
                e_hidden_lo(e)

            e_turned_lo(turn(0))
            stage(turn(0))
            stage(turn(1))
            with dve.Fori(1, E // 2 - 1) as i:
                for b in range(2):
                    stage(Turn(i, b))
            stage(turn(E - 2))
            stage(turn(E - 1), turn_next=False)

        @block.tensor
        def _(pe):
            def products(psum, pairs, first=True, final=True):
                for n, (lh, ll, rh, rl) in enumerate(pairs):
                    pe.matmul(psum, lh, rh, start=first and n == 0, stop=False)
                    pe.matmul(psum, lh, rl, start=False, stop=False)
                    ins = pe.matmul(psum, ll, rh, start=False, stop=final and n == len(pairs) - 1)
                return ins

            def turn_half(n, src, half, small=None):
                pe.wait_ge(xt_lo_made, 2 * n + half) if not (isinstance(n, int) and n == half == 0) else None
                for h in range(2):
                    for j in range(J):
                        at = (2 * half + h) * P
                        ins = pe.transpose(ptr[:, h, j * P:(j + 1) * P], src[:, j, at:at + P], ident[:])
                if small is not None:
                    for j in range(J):
                        ins = pe.transpose(ppos[0:3, j * P:(j + 1) * P], small[:, j, :], ident[:])
                ins.then_inc(turned, 1)

            def dots(s, r, hi, lo, row):
                at = slice(r * P, (r + 1) * P)
                products(pmm[r % 2][:], [(proj_hi[:, d, at], proj_lo[:, d, at], hi[:, d, :], lo[:, d, :])
                                         for d in range(HB)], final=False)
                pe.matmul(pmm[r % 2][:], corr_row[:, at], row[:], start=False, stop=True).then_inc(dot_done, 1)

            def dense_dots(g):
                pe.wait_ge(xt_lo_made, 2 * (g.n + 2) + 2)
                pe.wait_ge(norm_row_made, g.n + 2)
                for r in range(HB):
                    if r < 2:
                        at_least(pe, hid_made, IB * g.n)
                        pe.wait_ge(exp_done, HB * (g.n + 1) + r - 1)
                    else:
                        pe.wait_ge(exp_done, HB * (g.n + 1) + r - 1)
                    dots(1 + g.n, r, xt_hi[g.b], xt_lo[g.b], norm_row[g.b])

            def gate_up(g, i):
                for m, done in ((0, gate_done), (1, up_done)):
                    if i == 0:
                        pe.wait_ge(exp_done, HB * (g.n + 2) - 1 + m)
                    else:
                        pe.wait_ge(hid_made, IB * g.n + 1)
                    at = [slice(m * HB * I + h * I + i * P, m * HB * I + h * I + (i + 1) * P) for h in range(HB)]
                    products(pmm[m][:], [(sgu_hi[:, at[h]], sgu_lo[:, at[h]], xt_hi[g.b][:, h, :],
                                          xt_lo[g.b][:, h, :]) for h in range(HB)]).then_inc(done, 1)

            def logits(g):
                pe.wait_ge(xt_lo_made, 2 * (g.n + 2) + 2)
                at_least(pe, logit_made, g.n)
                for j in range(J):
                    at = slice(j * P, (j + 1) * P)
                    for h in range(HB):
                        for part in (xt_hi, xt_lo):
                            ins = pe.matmul(plog[:, at], part[g.b][:, h, at], router[:, h, :],
                                            start=(h == 0 and part is xt_hi),
                                            stop=(h == HB - 1 and part is xt_lo))
                ins.then_inc(logits_done, 1)

            def positions(g):
                pe.wait_ge(chosen_made, g.n + 1)
                pe.wait_ge(norm_row_made, g.n + 2)
                at_least(pe, slots_made, g.n)
                for j in range(J):
                    at = ppos[:, j * E:(j + 1) * E]
                    pe.matmul(at, before[:], chosen[:, j, :], start=True, stop=False)
                    for k in range(j):
                        pe.matmul(at, ones[:], chosen[:, k, :], start=False, stop=False)
                    ins = pe.matmul(at, ones[:], earlier[g.b][:], start=False, stop=True)
                ins.then_inc(pos_done, 1)

            def output(g, j):
                at = slice(j * P, (j + 1) * P)
                pe.wait_ge(feat_lo_made, HB * (g.n + 2))
                pe.wait_ge(hid_lo_made, IB * (g.n + 1))
                pe.wait_ge(out_free, J * g.n + j + 1)
                products(pout[j % 2][:], [(feat_hi[:, r, at], feat_lo[:, r, at], wt_hi[:, r, :], wt_lo[:, r, :])
                                          for r in range(HB)], final=False)
                products(pout[j % 2][:], [(shid_hi[:, i, at], shid_lo[:, i, at], sdn_hi[:, i * H:(i + 1) * H],
                                           sdn_lo[:, i * H:(i + 1) * H]) for i in range(IB)],
                         first=False).then_inc(out_done, 1)

            def group(g, last=False):
                nxt = g.next()
                dense_dots(g)
                if not last:
                    pe.wait_ge(xn_made, nxt.n + 1)
                    pe.wait_ge(norm3_made, nxt.n + 2)
                    turn_half(nxt.n + 2, xn, 0)
                gate_up(g, 0)
                if not last:
                    at_least(pe, slots_made, nxt.n)
                    turn_half(nxt.n + 2, xn, 1, norm3)
                gate_up(g, 1)
                if not last:
                    logits(nxt)
                output(g, 0)
                output(g, 1)
                if last:
                    pe.wait_ge(slot_rows_loaded, 16)
                    pe.wait_ge(logit_made, GROUPS)
                    pe.transpose(plog[:, 0:P], slot_rows, ident[:]).then_inc(slot_rows_turned, 1)
                else:
                    positions(nxt)
                output(g, 2)
                output(g, 3)

            pe.wait_ge(consts_made, 1)
            pe.wait_ge(xis_loaded, 16)
            pe.transpose(ppos[:, 0:HB], xis_row[:], ident[0:HB, 0:HB]).then_inc(xis_turned, 1)
            pe.wait_ge(proj_scaled, 1)
            turn_half(0, xbuf[1], 0)
            pe.wait_ge(corr3_made, 1)
            for r in range(HB):
                ins = pe.transpose(ppos[0:3, r * P:(r + 1) * P], corr3[:, r, :], ident[:])
            ins.then_inc(corr_turned, 1)
            turn_half(0, xbuf[1], 1)
            pe.wait_ge(norm3_made, 1)
            turn_half(1, xn, 0)
            pe.wait_ge(corr_row_made, 1)
            turn_half(1, xn, 1, norm3)
            pe.wait_ge(xt_lo_made, 4)
            pe.wait_ge(norm_row_made, 1)
            for r in range(HB):
                if r >= 2:
                    pe.wait_ge(exp_done, r - 1)
                dots(0, r, xt_hi[1], xt_lo[1], norm_row[1])
            pe.wait_ge(xn_made, 1)
            pe.wait_ge(norm3_made, 2)
            turn_half(2, xn, 0)
            turn_half(2, xn, 1, norm3)
            pe.wait_ge(router_made, 1)
            logits(turn(0))
            positions(turn(0))
            pe.wait_ge(shared_lo_made, 2)
            group(turn(0))
            group(turn(1))
            with pe.Fori(1, GROUPS // 2 - 1) as i:
                for b in range(2):
                    group(Turn(i, b))
            group(turn(GROUPS - 2))
            group(turn(GROUPS - 1), last=True)

            def e_turn(e):
                pe.wait_ge(gathered[e.b], 16 * CB * (e.i + 1))
                at_least(pe, e_xt_lo_made, e.n)
                for h in range(HB):
                    for c in range(CB):
                        ins = pe.transpose(ptr_e[:, h, c * P:(c + 1) * P], xe[e.b][:, c, h * P:(h + 1) * P],
                                           ident[:])
                ins.then_inc(e_turned, 1)

            def e_gate_up(e):
                pe.wait_ge(e_xt_lo_made, e.n + 1)
                pe.wait_ge(egu_lo_made, e.n + 1)
                at_least(pe, e_hid_made, e.n)
                for m, done in ((0, e_gate_done), (1, e_up_done)):
                    for i in range(IB):
                        at = [slice(m * HB * I + h * I + i * P, m * HB * I + h * I + (i + 1) * P)
                              for h in range(HB)]
                        ins = products(pmm[m][:, i * CAP:(i + 1) * CAP], [
                            (egu_hi[e.b][:, at[h]], egu_lo[e.b][:, at[h]], xt_hi[e.b][:, h, 0:CAP],
                             xt_lo[e.b][:, h, 0:CAP]) for h in range(HB)])
                    ins.then_inc(done, 1)

            def e_down(e):
                pe.wait_ge(e_hid_lo_made, e.n + 1)
                pe.wait_ge(edn_lo_made, e.n + 1)
                for c in range(CB):
                    at_least(pe, e_out_made, CB * (e.n - 1) + c + 1)
                    at = slice(c * P, (c + 1) * P)
                    products(pout[c][:], [
                        (hid_hi[:, e.b, i, at], hid_lo[:, e.b, i, at], edn_hi[e.b][:, i * H:(i + 1) * H],
                         edn_lo[e.b][:, i * H:(i + 1) * H]) for i in range(IB)]).then_inc(down_done, 1)

            e_turn(turn(0))
            e_turn(turn(1))
            e_gate_up(turn(0))
            pe.wait_ge(out_free, 2 + J * GROUPS)
            e_turn(turn(2))
            e_gate_up(turn(1))
            e_down(turn(0))
            with pe.Fori(1, E // 2 - 1) as i:
                for b in range(2):
                    e = Turn(i, b)
                    e_turn(e.next())
                    e_gate_up(e)
                    e_down(e.prev())
            e_turn(turn(E - 1))
            e_gate_up(turn(E - 2))
            e_down(turn(E - 3))
            e_gate_up(turn(E - 1))
            e_down(turn(E - 2))
            e_down(turn(E - 1))

        @block.gpsimd
        def _(pool):
            steps = [0]

            def step(ins):
                ins.then_inc(pool_step, 1)
                steps[0] += 1

            def wait_apart(sem, value):
                pool.wait_ge(sem, value)
                pool.tensor_tensor(pool_sink[:], pool_carrier[:], pool_carrier[:], ALU.add)

            step(pool.memset(pool_carrier[:], 0.0))
            step(pool.memset(ident[:], 0.0))
            step(pool.memset(before[:], 1.0))
            step(pool.memset(ones[:], 1.0))
            step(pool.memset(lower[:], 1.0))
            step(pool.memset(zeros, 0.0))
            step(pool.iota(token_ids_i[:], [[P, GROUPS * J]], base=0, channel_multiplier=1))
            step(pool.iota(no_token_i, [[1, CAP]], base=TOKENS, channel_multiplier=0))
            step(pool.iota(expert_base_i[:], [[-CAP, E]], base=OUTSIDE, channel_multiplier=0))
            pool.wait_ge(pool_step, steps[0])
            step(pool.affine_select(out=ident[:], in_=ident[:], compare_op=ALU.not_equal, fill=1.0, base=0,
                                    pattern=[[-1, P]], channel_multiplier=1))
            step(pool.affine_select(out=before[:], in_=before[:], compare_op=ALU.is_gt, fill=0.0, base=0,
                                    pattern=[[1, P]], channel_multiplier=-1))
            step(pool.affine_select(out=lower[:], in_=lower[:], compare_op=ALU.is_gt, fill=0.0, base=0,
                                    pattern=[[1, RG], [-1, RG]], channel_multiplier=0))
            step(pool.tensor_copy(token_ids[:], token_ids_i[:]))
            step(pool.tensor_copy(no_token, no_token_i))
            pool.wait_ge(pool_step, steps[0])
            pool.tensor_copy(expert_base[:], expert_base_i[:]).then_inc(consts_made, 1)

            pool.wait_ge(table_made, 16 * (1 + 2 * SPARE // P))
            last_slot = pool.to_reg(SLOTS - 1)
            last_row = pool.to_reg(TOKENS + SPARE - 1)
            with pool.Fori(0, GROUPS // 2) as i:
                for b in range(2):
                    g = Turn(i, b)
                    pool.wait_ge(slots_made, g.n + 1)
                    pool.tensor_copy(ids[b][:], token_ids[:, bass.ds(J * g.n, J)]).then_inc(idx_copied, 1)
                    wait_apart(idx_copied, g.n + 1)
                    for j in range(J):
                        for k in range(K):
                            pool.indirect_dma_start(
                                out=slot_token, out_offset=bass.IndirectOffsetOnAxis(
                                    ap=slots[b][:, j, k:k + 1], axis=0),
                                in_=ids[b][:, j:j + 1], in_offset=None, bounds_check=last_slot,
                                oob_is_err=False).then_inc(scattered[b], 16)

            def gather(e, copied):
                pool.tensor_copy(gidx[e.b][:], slot_cols[:, bass.ds(CB * e.n, CB)]).then_inc(idx_copied, 1)
                wait_apart(idx_copied, copied)
                for c in range(CB):
                    pool.indirect_dma_start(
                        out=xe[e.b][:, c, :], out_offset=None, in_=rows,
                        in_offset=bass.IndirectOffsetOnAxis(ap=gidx[e.b][:, c:c + 1], axis=0),
                        bounds_check=last_row, oob_is_err=True).then_inc(gathered[e.b], 16)

            def add_rows(e, copied):
                at_least(pool, added, 16 * CB * e.n)
                pool.wait_ge(e_out_made, CB * (e.n + 1))
                pool.tensor_copy(sidx[e.b][:], slot_cols[:, bass.ds(CB * e.n, CB)]).then_inc(idx_copied, 1)
                wait_apart(idx_copied, copied)
                for c in range(CB):
                    pool.indirect_dma_start(
                        out=out, out_offset=bass.IndirectOffsetOnAxis(ap=sidx[e.b][:, c:c + 1], axis=0),
                        in_=outs[e.b][:, c, :], in_offset=None, bounds_check=last_row,
                        oob_is_err=True, compute_op=ALU.add).then_inc(added, 16)

            pool.wait_ge(slot_cols_made, 1)
            pool.wait_ge(xn_stored, 16 * GROUPS)
            pool.wait_ge(w_stored, 16 * GROUPS)
            pool.wait_ge(out_free, 2 + J * (GROUPS - 1))
            gather(turn(0), GROUPS + 1)
            pool.wait_ge(out_free, 2 + J * GROUPS)
            gather(turn(1), GROUPS + 2)
            pool.wait_ge(slot_w_made, 1)
            gather(turn(2), GROUPS + 3)
            for b in range(2):
                pool.wait_ge(out_stored[b], 16 * GROUPS)

            def stage(e):
                pool.wait_ge(slot_w_made, e.n + 1)
                gather(Turn(e.i + 1, e.b), GROUPS + 2 * e.n + 2)
                add_rows(e.prev(), GROUPS + 2 * e.n + 3)

            stage(turn(1))
            with pool.Fori(1, E // 2 - 1) as i:
                for b in range(2):
                    stage(Turn(i, b))
            for n in (E - 3, E - 2, E - 1):
                add_rows(turn(n), GROUPS + E + n + 1)
            pool.wait_ge(added, 16 * CB * E)


_INS = ['L0_attn_x', 'L0_attn_input_weights', 'L0_attn_xis', 'L0_attn_proj_matrix', 'L0_ffn_router_w',
        'L0_ffn_gate_w', 'L0_ffn_up_w', 'L0_ffn_down_w', 'L0_ffn_shared_gate_w', 'L0_ffn_shared_up_w',
        'L0_ffn_shared_down_w']


def kernel(**inputs):
    import numpy as _np
    import concourse.bacc as _bacc
    from concourse import mybir as _mybir
    from concourse.bass_utils import run_bass_kernel_spmd as _run

    nc = _bacc.Bacc("TRN2", target_bir_lowering=False, num_devices=1)
    arrays, args = {}, []
    for name in _INS:
        a = _np.ascontiguousarray(inputs[name])
        arrays[f"in_{name}_dram"] = a
        args.append(nc.dram_tensor(f"in_{name}_dram", a.shape, _mybir.dt.from_np(a.dtype), kind="ExternalInput").ap())
    args.append(nc.dram_tensor("out_0_dram", (TOKENS + SPARE, H), _mybir.dt.from_np(_np.dtype("float32")),
                               kind="ExternalOutput").ap())
    build(nc, *args)
    r = _run(nc, [arrays], core_ids=[0])
    return r.results[0]["out_0_dram"][:TOKENS].reshape(4, 2048, H)
```

```python
from contextlib import ExitStack

import concourse.bass as bass
from concourse import mybir

ALU = mybir.AluOpType
ACT = mybir.ActivationFunctionType
F32 = mybir.dt.float32
F32R = mybir.dt.float32r
BF16 = mybir.dt.bfloat16
I32 = mybir.dt.int32
U32 = mybir.dt.uint32
AX_X = mybir.AxisListType.X

P = 128
H = 512
HB = H // P
TOKENS = 8192
GROUP = 512
J = GROUP // P
GROUPS = TOKENS // GROUP
E = 64
EG = 8
RG = E // EG
TOP_GROUPS = 4
K = 8
CAP = 256
CB = CAP // P
I = 256
IB = I // P
SCALE = 2.5
EPS = 1e-5
RSQRT_SEED = 0x5F3759DF
SLOTS = E * CAP
SPARE = CAP
ROW = H + E
GU = 2 * HB * I
DN = IB * H
OUTSIDE = 2 * SLOTS
SCATTER = 16 * J * K


class Turn:

    def __init__(self, i, b):
        self.i, self.b = i, b
        self.n = 2 * i + b

    def next(self):
        return Turn(self.i, 1) if self.b == 0 else Turn(self.i + 1, 0)

    def prev(self):
        return Turn(self.i, 0) if self.b == 1 else Turn(self.i - 1, 1)


def turn(n):
    return Turn(n // 2, n % 2)


def at_least(eng, sem, value):
    if not (isinstance(value, int) and value <= 0):
        eng.wait_ge(sem, value)


def build(nc, x, iw, xis, proj, router_w, gate_w, up_w, down_w, sgate_w, sup_w, sdown_w, out):
    with ExitStack() as ctx:
        def sb(name, shape, dt=F32):
            return ctx.enter_context(nc.sbuf_tensor(name, shape, dt))

        def ps(name, shape):
            return ctx.enter_context(nc.psum_tensor(name, shape, F32))

        def sem(name):
            return ctx.enter_context(nc.semaphore(name))

        rows = nc.dram_tensor("rows", [TOKENS + SPARE, ROW], F32).ap()
        slot_token = nc.dram_tensor("slot_token", [SLOTS, 1], F32).ap()

        ident = sb("ident", [P, P])
        before = sb("before", [P, P], BF16)
        ones = sb("ones", [P, P], BF16)
        lower = sb("lower", [P, RG, RG])
        expert_base = sb("expert_base", [P, E])
        token_ids_i = sb("token_ids_i", [P, GROUPS * J], I32)
        token_ids = sb("token_ids", [P, GROUPS * J])
        expert_base_i = sb("expert_base_i", [P, E], I32)
        proj_hi = sb("proj_hi", [P, HB, H], F32R)
        proj_lo = sb("proj_lo", [P, HB, H], F32R)
        wt_hi = sb("wt_hi", [P, HB, H], F32R)
        wt_lo = sb("wt_lo", [P, HB, H], F32R)
        sgu_hi = sb("sgu_hi", [P, GU], F32R)
        sgu_lo = sb("sgu_lo", [P, GU], F32R)
        sdn_hi = sb("sdn_hi", [P, DN], F32R)
        sdn_lo = sb("sdn_lo", [P, DN], F32R)
        router = sb("router", [P, HB, 2 * E], F32R)
        xis_row = sb("xis_row", [HB, P])
        ab = sb("ab", [P, HB])
        ab2 = sb("ab2", [P, HB])
        corr = sb("corr", [P, HB])
        corr_r = sb("corr_r", [P, HB], F32R)
        corr3 = sb("corr3", [P, HB, 3])
        corr_row = sb("corr_row", [3, H], F32R)
        xbuf = [sb(f"xbuf{b}", [P, J, H]) for b in range(2)]
        xn = sb("xn", [P, J, H])
        xt_hi = [sb(f"xt_hi{b}", [P, HB, GROUP], F32R) for b in range(2)]
        xt_lo = [sb(f"xt_lo{b}", [P, HB, GROUP], F32R) for b in range(2)]
        wait_carrier = sb("wait_carrier", [P, 1])
        pool_carrier = sb("pool_carrier", [P, 1])
        pool_sink = sb("pool_sink", [P, 1])
        stats = sb("stats", [P, J, 6])
        mean_var = sb("mean_var", [P, J, 2])
        var_eps = sb("var_eps", [P, J])
        rstd = sb("rstd", [P, J])
        rstd2 = sb("rstd2", [P, J])
        norm = sb("norm", [P, J])
        norm_r = sb("norm_r", [P, J], F32R)
        iw_norm = sb("iw_norm", [P, HB])
        norm3 = sb("norm3", [P, J, 3])
        norm_row = [sb(f"norm_row{b}", [3, GROUP], F32R) for b in range(2)]
        feat = sb("feat", [P, 2, GROUP])
        feat_hi = sb("feat_hi", [P, HB, GROUP], F32R)
        feat_lo = sb("feat_lo", [P, HB, GROUP], F32R)
        gate_t = sb("gate_t", [P, GROUP])
        gate_a = sb("gate_a", [P, GROUP])
        hid = sb("hid", [P, GROUP])
        hid_hi = sb("hid_hi", [P, 2, IB, CAP], F32R)
        hid_lo = sb("hid_lo", [P, 2, IB, CAP], F32R)
        shid_hi = hid_hi[:].rearrange("p a b c -> p (a b c)").rearrange("p (i t) -> p i t", i=IB)
        shid_lo = hid_lo[:].rearrange("p a b c -> p (a b c)").rearrange("p (i t) -> p i t", i=IB)
        outs = [sb(f"outs{b}", [P, 2, H]) for b in range(2)]
        logit = sb("logit", [P, J, E])
        expn = sb("expn", [P, J, E])
        score = sb("score", [P, J, E])
        gmax = sb("gmax", [P, J, RG])
        beats = sb("beats", [P, J, RG, 2 * RG])
        rank = sb("rank", [P, J * RG])
        masked = sb("masked", [P, J, E])
        top = sb("top", [P, J, K])
        taken = sb("taken", [P, J, E])
        chosen = sb("chosen", [P, J, E], BF16)
        wsum = sb("wsum", [P, J])
        weight = sb("weight", [P, J, E])
        nchosen = sb("nchosen", [P, E])
        earlier = [sb(f"earlier{b}", [P, E], BF16) for b in range(2)]
        key = sb("key", [P, J, E])
        key8 = sb("key8", [P, J, K])
        slots = [sb(f"slots{b}", [P, J, K], U32) for b in range(2)]
        ids = [sb(f"ids{b}", [P, J]) for b in range(2)]
        raw = [sb(f"raw{b}", [P, GU + DN]) for b in range(2)]
        slot_rows = key[:].rearrange("p j e -> p (j e)")[:, 0:P]
        slot_cols = sb("slot_cols", [P, P], U32)
        gidx = [sb(f"gidx{b}", [P, CB], U32) for b in range(2)]
        sidx = [sb(f"sidx{b}", [P, CB], U32) for b in range(2)]
        slot_w = [sb(f"slot_w{b}", [P, CB]) for b in range(2)]
        router_raw = gate_a[:, 0:HB * E].rearrange("p (c e) -> p c e", c=HB)
        square = hid
        iw_raw = raw[1][:, 0:HB * H].rearrange("p (c d) -> p c d", c=HB)
        zeros = outs[0][:].rearrange("p a h -> p (a h)")[:, 0:ROW]
        no_token_i = outs[1][0:E, 0, 0:CAP].bitcast(I32)
        no_token = outs[1][0:E, 1, 0:CAP]
        xe = [xbuf[b][:].rearrange("p j h -> p (j h)")[:, 0:CB * ROW].rearrange("p (c h) -> p c h", c=CB)
              for b in range(2)]
        egu_hi = [proj_hi[:].rearrange("p a b -> p (a b)"), sgu_hi[:, :]]
        egu_lo = [proj_lo[:].rearrange("p a b -> p (a b)"), sgu_lo[:, :]]
        edn_hi = [sdn_hi[:, :], feat_hi[:, 0:IB, :].rearrange("p a b -> p (a b)")]
        edn_lo = [sdn_lo[:, :], feat_lo[:, 0:IB, :].rearrange("p a b -> p (a b)")]

        ptr = ps("ptr", [P, 2, 512])
        pmm2 = ps("pmm", [P, 2, 512])
        pout2 = ps("pout", [P, 2, 512])
        pmm = [pmm2[:, b, :] for b in range(2)]
        pout = [pout2[:, b, :] for b in range(2)]
        plog = ps("plog", [P, 512])
        ppos = ps("ppos", [P, 512])
        ptr_e = ptr[:].rearrange("p a b -> p (a b)").rearrange("p (h c) -> p h c", h=HB)

        ident_made = sem("ident_made")
        consts_made = sem("consts_made")
        ab_made = sem("ab_made")
        iw_norm_made = sem("iw_norm_made")
        pool_step = sem("pool_step")
        xis_loaded = sem("xis_loaded")
        proj_loaded = sem("proj_loaded")
        iw_loaded = sem("iw_loaded")
        router_loaded = sem("router_loaded")
        table_made = sem("table_made")
        xis_turned = sem("xis_turned")
        proj_scaled = sem("proj_scaled")
        corr3_made = sem("corr3_made")
        corr_turned = sem("corr_turned")
        corr_row_made = sem("corr_row_made")
        ab2_exp = sem("ab2_exp")
        ab2_made = sem("ab2_made")
        router_hi_made = sem("router_hi_made")
        router_made = sem("router_made")
        shared_hi_made = sem("shared_hi_made")
        shared_lo_made = sem("shared_lo_made")
        vec_step = sem("vec_step")
        x_loaded = [sem(f"x_loaded{b}") for b in range(2)]
        moments_made = sem("moments_made")
        xn_made = sem("xn_made")
        norm3_made = sem("norm3_made")
        xn_stored = sem("xn_stored")
        w_made = sem("w_made")
        w_stored = sem("w_stored")
        turned = sem("turned")
        xt_hi_made = sem("xt_hi_made")
        xt_lo_made = sem("xt_lo_made")
        norm_row_made = sem("norm_row_made")
        dot_done = sem("dot_done")
        exp_done = sem("exp_done")
        feat_hi_made = sem("feat_hi_made")
        feat_lo_made = sem("feat_lo_made")
        gate_done = sem("gate_done")
        up_done = sem("up_done")
        tanh_done = sem("tanh_done")
        hid_made = sem("hid_made")
        hid_hi_made = sem("hid_hi_made")
        hid_lo_made = sem("hid_lo_made")
        out_done = sem("out_done")
        residual_loaded = [sem(f"residual_loaded{b}") for b in range(2)]
        out_free = sem("out_free")
        out_stored = [sem(f"out_stored{b}") for b in range(2)]
        logits_done = sem("logits_done")
        logit_made = sem("logit_made")
        expn_made = sem("expn_made")
        chosen_made = sem("chosen_made")
        pos_done = sem("pos_done")
        slots_made = sem("slots_made")
        scattered = [sem(f"scattered{b}") for b in range(2)]
        slot_rows_loaded = sem("slot_rows_loaded")
        slot_rows_turned = sem("slot_rows_turned")
        slot_cols_made = sem("slot_cols_made")
        gu_loaded = [sem(f"gu_loaded{b}") for b in range(2)]
        dn_loaded = [sem(f"dn_loaded{b}") for b in range(2)]
        idx_copied = sem("idx_copied")
        gathered = [sem(f"gathered{b}") for b in range(2)]
        slot_w_made = sem("slot_w_made")
        e_turned = sem("e_turned")
        e_xt_hi_made = sem("e_xt_hi_made")
        e_xt_lo_made = sem("e_xt_lo_made")
        egu_hi_made = sem("egu_hi_made")
        egu_lo_made = sem("egu_lo_made")
        edn_hi_made = sem("edn_hi_made")
        edn_lo_made = sem("edn_lo_made")
        e_gate_done = sem("e_gate_done")
        e_up_done = sem("e_up_done")
        silu_done = sem("silu_done")
        e_hid_made = sem("e_hid_made")
        e_hid_hi_made = sem("e_hid_hi_made")
        e_hid_lo_made = sem("e_hid_lo_made")
        down_done = sem("down_done")
        e_out_made = sem("e_out_made")
        added = sem("added")

        x_groups = x.rearrange("b s h -> (b s) h").rearrange("(g j p) h -> g p j h", j=J, p=P)
        x_halves = x.rearrange("b s h -> (b s) h").rearrange("(g a j p) h -> g a p j h", a=2, j=2, p=P)
        rows_groups = rows[0:TOKENS, :].rearrange("(g j p) h -> g p j h", j=J, p=P)
        out_halves = out[0:TOKENS, :].rearrange("(g a j p) h -> g a p j h", a=2, j=2, p=P)

        block = ctx.enter_context(nc.Block())

        @block.sync
        def _(sp):
            def load_x(g):
                sp.dma_start(xbuf[g.b][:], x_groups[g.n]).then_inc(x_loaded[g.b], 16)

            def load_gate_up(b, gate, up):
                sp.dma_start(raw[b][:, 0:GU // 2].rearrange("p (c i) -> p c i", c=HB),
                             gate.rearrange("(c p) i -> p c i", p=P)).then_inc(gu_loaded[b], 16)
                sp.dma_start(raw[b][:, GU // 2:GU].rearrange("p (c i) -> p c i", c=HB),
                             up.rearrange("(c p) i -> p c i", p=P)).then_inc(gu_loaded[b], 16)

            def load_down(b, down):
                sp.dma_start(raw[b][:, GU:].rearrange("p (c h) -> p c h", c=IB),
                             down.rearrange("(c p) h -> p c h", p=P)).then_inc(dn_loaded[b], 16)

            def store_xn(g):
                sp.wait_ge(xn_made, g.n + 1)
                sp.dma_start(rows_groups[g.n][:, :, 0:H], xn[:]).then_inc(xn_stored, 16)

            def store_w(g):
                sp.wait_ge(w_made, g.n + 1)
                sp.dma_start(rows_groups[g.n][:, :, H:ROW], weight[:]).then_inc(w_stored, 16)

            def load_residual(g):
                for a in range(2):
                    at_least(sp, out_stored[a], 16 * g.n)
                    sp.dma_start(outs[a][:], x_halves[g.n, a]).then_inc(residual_loaded[a], 16)

            def store_out(g, a):
                sp.wait_ge(out_free, 2 + J * g.n + 2 * a + 2)
                sp.dma_start(out_halves[g.n, a], outs[a][:]).then_inc(out_stored[a], 16)

            def group(g, load=True, last=False):
                load_residual(g)
                if load:
                    load_x(Turn(g.i + 1, g.b))
                if not last:
                    store_xn(g.next())
                store_out(g, 0)
                if not last:
                    store_w(g.next())
                store_out(g, 1)

            sp.dma_start(xis_row[:], xis.rearrange("(c p) -> c p", p=P)).then_inc(xis_loaded, 16)
            load_x(turn(0))
            sp.dma_start(xbuf[1][:], proj.rearrange("(c p) d -> p c d", p=P)).then_inc(proj_loaded, 16)
            sp.dma_start(iw_raw, iw.rearrange("(c p) d -> p c d", p=P)).then_inc(iw_loaded, 16)
            sp.dma_start(router_raw, router_w.rearrange("(c p) e -> p c e", p=P)).then_inc(router_loaded, 16)
            load_gate_up(0, sgate_w, sup_w)
            load_down(0, sdown_w)
            sp.wait_ge(consts_made, 1)
            sp.dma_start(slot_token.rearrange("(e s) o -> e (s o)", s=CAP), no_token).then_inc(table_made, 16)
            for c in range(SPARE // P):
                at = slice(TOKENS + c * P, TOKENS + (c + 1) * P)
                sp.dma_start(rows[at, :], zeros).then_inc(table_made, 16)
                sp.dma_start(out[at, :], zeros[:, 0:H]).then_inc(table_made, 16)
            sp.wait_ge(turned, 2)
            load_x(turn(1))
            store_xn(turn(0))
            sp.wait_ge(turned, 6)
            load_gate_up(1, gate_w[1], up_w[1])
            load_down(1, down_w[1])
            store_w(turn(0))
            sp.wait_ge(shared_lo_made, 2)
            load_gate_up(0, gate_w[0], up_w[0])
            load_down(0, down_w[0])
            sp.wait_ge(table_made, 16 * (1 + 2 * SPARE // P))
            group(turn(0))
            group(turn(1))
            with sp.Fori(1, GROUPS // 2 - 1) as i:
                for b in range(2):
                    group(Turn(i, b))
            group(turn(GROUPS - 2), load=False)
            load_residual(turn(GROUPS - 1))
            for b in range(2):
                sp.wait_ge(scattered[b], SCATTER * GROUPS // 2)
            sp.dma_start(slot_rows, slot_token.rearrange("(q p) o -> q (p o)", p=P)).then_inc(
                slot_rows_loaded, 16)
            for a in range(2):
                store_out(turn(GROUPS - 1), a)

            def refill(e):
                b = e.b
                sp.wait_ge(egu_hi_made, e.n - 1)
                sp.wait_ge(egu_lo_made, e.n - 1)
                load_gate_up(b, gate_w[e.n], up_w[e.n])
                sp.wait_ge(edn_hi_made, e.n - 1)
                sp.wait_ge(edn_lo_made, e.n - 1)
                load_down(b, down_w[e.n])

            with sp.Fori(1, E // 2) as i:
                for b in range(2):
                    refill(Turn(i, b))

        @block.scalar
        def _(act):
            copy = ACT.Copy

            def features(s, r, hi, scale=None):
                act.wait_ge(dot_done, HB * s + r + 1)
                at_least(act, feat_lo_made, HB * s + r - 1)
                act.activation(feat[:, r % 2], pmm[r % 2], ACT.Exp).then_inc(exp_done, 1)
                act.wait_ge(exp_done, HB * s + r + 1)
                if scale is None:
                    act.activation(hi[:, r, :], feat[:, r % 2], copy).then_inc(feat_hi_made, 1)
                else:
                    act.activation(hi[:, r, :], feat[:, r % 2], copy, scale=scale).then_inc(feat_hi_made, 1)

            def hidden(g, i):
                act.wait_ge(gate_done, IB * g.n + i + 1)
                at_least(act, hid_made, IB * g.n + i)
                act.activation(gate_t[:], pmm[0], ACT.Tanh, scale=0.5).then_inc(tanh_done, 1)

            def hidden_hi(g, i):
                act.wait_ge(hid_made, IB * g.n + i + 1)
                act.activation(shid_hi[:, i, :], hid[:], copy).then_inc(hid_hi_made, 1)

            def exp_logits(g):
                act.wait_ge(logit_made, g.n + 1)
                act.activation(expn[:], logit[:], ACT.Exp, scale=-1.0).then_inc(expn_made, 1)

            def hi_half(n, half, dst, psum=ptr):
                act.wait_ge(turned, 2 * n + half + 1)
                act.activation(dst[:, 2 * half:2 * half + 2, :], psum[:], copy).then_inc(xt_hi_made, 1)

            def hi_norm(g):
                act.activation(norm_row[g.b][:], ppos[0:3, :], copy).then_inc(norm_row_made, 1)

            def group(g, last=False):
                nxt = g.next()
                for r in range(HB):
                    features(1 + g.n, r, feat_hi)
                if not last:
                    hi_half(nxt.n + 2, 0, xt_hi[nxt.b])
                hidden(g, 0)
                hidden_hi(g, 0)
                if not last:
                    hi_half(nxt.n + 2, 1, xt_hi[nxt.b])
                    hi_norm(nxt)
                hidden(g, 1)
                hidden_hi(g, 1)
                if not last:
                    exp_logits(nxt)

            act.wait_ge(ab_made, 1)
            act.activation(ab2[:], ab[:], ACT.Exp, scale=2.0).then_inc(ab2_exp, 1)
            act.wait_ge(proj_loaded, 16)
            for r in range(HB):
                ins = act.activation(xbuf[1][:, r, :], xbuf[1][:, r, :], copy, scale=ab[:, r:r + 1])
            ins.then_inc(proj_scaled, 1)
            act.wait_ge(iw_loaded, 16)
            for r in range(HB):
                ins = act.activation(square[:] if r % 2 == 0 else gate_t[:], iw_raw[:, r, :], ACT.Square,
                                     accum_out=iw_norm[:, r:r + 1])
                if r >= 1:
                    ins.then_inc(iw_norm_made, 1)
                    act.wait_ge(iw_norm_made, r)
            for half in range(2):
                hi_half(0, half, proj_hi, (ptr, pmm2)[half])
            act.wait_ge(corr_turned, 1)
            act.activation(corr_row[:], ppos[0:3, :], copy).then_inc(corr_row_made, 1)
            act.wait_ge(router_loaded, 16)
            act.activation(router[:, :, 0:E], router_raw, copy).then_inc(router_hi_made, 1)
            for half in range(2):
                hi_half(1, half, xt_hi[0], (pout2, ptr)[half])
            hi_norm(turn(0))
            for half in range(2):
                hi_half(2, half, xt_hi[1], (pout2, ptr)[half])
            hi_norm(turn(1))
            exp_logits(turn(0))
            act.wait_ge(ab2_made, 1)
            for r in range(HB):
                features(0, r, wt_hi, scale=ab2[:, r:r + 1])
                if r == 1:
                    act.wait_ge(gu_loaded[0], 32)
                    act.activation(sgu_hi[:], raw[0][:, 0:GU], copy).then_inc(shared_hi_made, 1)
            act.wait_ge(dn_loaded[0], 16)
            act.activation(sdn_hi[:], raw[0][:, GU:], copy).then_inc(shared_hi_made, 1)
            group(turn(0))
            group(turn(1))
            with act.Fori(1, GROUPS // 2 - 1) as i:
                for b in range(2):
                    group(Turn(i, b))
            group(turn(GROUPS - 2))
            group(turn(GROUPS - 1), last=True)

            def gate_up_hi(e, at_start=False):
                if at_start:
                    act.wait_ge(dot_done, HB * (GROUPS + 1))
                act.wait_ge(gu_loaded[e.b], 32 * (e.i + (2 if e.b == 0 else 1)))
                act.activation(egu_hi[e.b], raw[e.b][:, 0:GU], copy).then_inc(egu_hi_made, 1)

            def down_hi(e):
                act.wait_ge(dn_loaded[e.b], 16 * (e.i + (2 if e.b == 0 else 1)))
                act.activation(edn_hi[e.b], raw[e.b][:, GU:], copy).then_inc(edn_hi_made, 1)

            def e_turned_hi(e):
                act.wait_ge(e_turned, e.n + 1)
                act.activation(xt_hi[e.b][:, :, 0:CAP], ptr_e, copy).then_inc(e_xt_hi_made, 1)

            def e_silu(e):
                act.wait_ge(e_gate_done, e.n + 1)
                at_least(act, e_hid_made, e.n)
                act.activation(gate_t[:], pmm[0], ACT.Silu).then_inc(silu_done, 1)

            def e_hidden_hi(e):
                act.wait_ge(e_hid_made, e.n + 1)
                act.activation(hid_hi[:, e.b].rearrange("p a b -> p (a b)"), hid[:], copy).then_inc(
                    e_hid_hi_made, 1)

            def e_out(e):
                act.wait_ge(slot_w_made, e.n + 1)
                at_least(act, added, 16 * CB * (e.n - 1))
                for c in range(CB):
                    act.wait_ge(down_done, CB * e.n + c + 1)
                    act.activation(outs[e.b][:, c], pout[c], copy, scale=slot_w[e.b][:, c:c + 1]).then_inc(
                        e_out_made, 1)

            def stage(e, turn_next=True, run=True, out_prev=True):
                if turn_next:
                    e_turned_hi(e.next())
                    gate_up_hi(e.next())
                if run:
                    e_silu(e)
                    down_hi(e)
                    e_hidden_hi(e)
                if out_prev:
                    e_out(e.prev())

            gate_up_hi(turn(0), at_start=True)
            e_turned_hi(turn(0))
            for b in range(2):
                act.wait_ge(out_stored[b], 16 * GROUPS)
            stage(turn(0), out_prev=False)
            stage(turn(1))
            with act.Fori(1, E // 2 - 1) as i:
                for b in range(2):
                    stage(Turn(i, b))
            stage(turn(E - 2))
            stage(turn(E - 1), turn_next=False)
            e_out(turn(E - 1))

        @block.vector
        def _(dve):
            steps = [0]

            def step(ins, base=0, apart=False):
                ins.then_inc(vec_step, 1)
                steps[0] += 1
                dve.wait_ge(vec_step, base + steps[0])
                if apart:
                    dve.memset(wait_carrier[:], 0.0)

            def split_norm(norm, base=0):
                step(dve.tensor_copy(norm_r[:], norm[:]), base)
                dve.tensor_copy(norm3[:, :, 0:2], norm_r[:].bitcast(F32).unsqueeze(2).to_broadcast([P, J, 2]))
                dve.tensor_tensor(norm3[:, :, 2], norm[:], norm_r[:].bitcast(F32), ALU.subtract).then_inc(
                    norm3_made, 1)

            def lo_half(n, half, hi, lo, psum=ptr):
                dve.wait_ge(xt_hi_made, 2 * n + half + 1)
                at = slice(2 * half, 2 * half + 2)
                dve.tensor_tensor(lo[:, at, :], psum[:], hi[:, at, :].bitcast(F32), ALU.subtract).then_inc(
                    xt_lo_made, 1)

            def features_lo(s, r, hi, lo, scale=1.0):
                dve.wait_ge(feat_hi_made, HB * s + r + 1)
                if isinstance(scale, float):
                    ins = dve.tensor_tensor(lo[:, r, :], feat[:, r % 2], hi[:, r, :].bitcast(F32), ALU.subtract)
                else:
                    ins = dve.scalar_tensor_tensor(out=lo[:, r, :], in0=feat[:, r % 2], scalar=scale,
                                                   in1=hi[:, r, :].bitcast(F32), op0=ALU.mult,
                                                   op1=ALU.subtract)
                ins.then_inc(feat_lo_made, 1)

            def moments(g):
                dve.wait_ge(x_loaded[g.b], 16 * (g.i + 1))
                for j in range(J):
                    ins = dve.bn_stats(stats[:, j, :], xbuf[g.b][:, j, :])
                ins.then_inc(moments_made, 1)

            def deviations(g, base):
                dve.wait_ge(moments_made, g.n + 1)
                dve.memset(wait_carrier[:], 0.0)
                for j in range(J):
                    ins = dve.bn_aggr(mean_var[:, j, :], stats[:, j, :])
                step(ins, base)
                step(dve.tensor_scalar(var_eps[:], mean_var[:, :, 1], EPS, None, ALU.add), base)
                step(dve.tensor_scalar(rstd2[:].bitcast(I32), var_eps[:].bitcast(I32), 1, None,
                                       ALU.arith_shift_right), base)
                step(dve.tensor_scalar(rstd[:].bitcast(I32), rstd2[:].bitcast(I32), -1.0,
                                       float(RSQRT_SEED), ALU.mult, ALU.add), base)
                for _ in range(3):
                    step(dve.tensor_tensor(rstd2[:], rstd[:], rstd[:], ALU.mult), base)
                    step(dve.scalar_tensor_tensor(out=rstd2[:], in0=rstd2[:], scalar=-0.5, in1=var_eps[:],
                                                  op0=ALU.mult, op1=ALU.mult), base)
                    step(dve.scalar_tensor_tensor(out=rstd[:], in0=rstd2[:], scalar=1.5, in1=rstd[:],
                                                  op0=ALU.add, op1=ALU.mult), base)

            def normalise(g, base):
                if not isinstance(g.n, int) or g.n > 0:
                    dve.wait_ge(turned, 2 * (g.n + 2))
                    dve.wait_ge(xn_stored, 16 * g.n)
                for j in range(J):
                    ins = dve.tensor_scalar(xn[:, j, :], xbuf[g.b][:, j, :], mean_var[:, j, 0:1],
                                            rstd[:, j:j + 1], ALU.subtract, ALU.mult)
                ins.then_inc(xn_made, 1)
                step(dve.tensor_tensor(rstd2[:], rstd[:], rstd[:], ALU.mult), base)
                step(dve.scalar_tensor_tensor(out=norm[:], in0=mean_var[:, :, 1], scalar=float(H),
                                              in1=rstd2[:], op0=ALU.mult, op1=ALU.mult), base)
                split_norm(norm, base)

            def rank_groups(g, base):
                lg = plog[:].rearrange("p (j a e) -> p j a e", j=J, a=2)
                dve.wait_ge(logits_done, g.n + 1)
                step(dve.tensor_copy(logit[:], lg[:, :, 0, :]), base)
                dve.tensor_tensor(logit[:], logit[:], lg[:, :, 1, :], ALU.add).then_inc(logit_made, 1)
                dve.wait_ge(expn_made, g.n + 1)
                step(dve.tensor_scalar(expn[:], expn[:], 1.0, None, ALU.add), base)
                step(dve.reciprocal(score[:], expn[:]), base)
                step(dve.tensor_reduce(gmax[:], score[:].rearrange("p j (g e) -> p (j g) e", e=EG), AX_X,
                                       ALU.max), base)
                other = gmax[:].unsqueeze(2).to_broadcast([P, J, RG, RG])
                own = gmax[:].unsqueeze(3).to_broadcast([P, J, RG, RG])
                dve.tensor_tensor(beats[:, :, :, 0:RG], other, own, ALU.is_gt)
                step(dve.tensor_tensor(beats[:, :, :, RG:], other, own, ALU.is_equal), base)
                step(dve.tensor_tensor(beats[:, :, :, RG:], beats[:, :, :, RG:],
                                       lower[:].unsqueeze(1).to_broadcast([P, J, RG, RG]), ALU.mult), base)
                step(dve.tensor_reduce(rank[:], beats[:].rearrange("p j g o -> p (j g) o"), AX_X, ALU.add), base)

            def choose(g, base):
                step(dve.scalar_tensor_tensor(
                    out=masked[:].rearrange("p j (g e) -> p (j g) e", e=EG),
                    in0=rank[:].unsqueeze(2).to_broadcast([P, J * RG, EG]), scalar=float(TOP_GROUPS),
                    in1=score[:].rearrange("p j (g e) -> p (j g) e", e=EG), op0=ALU.is_lt, op1=ALU.mult), base,
                    apart=True)
                for j in range(J):
                    ins = dve.max(top[:, j, :], masked[:, j, :])
                step(ins, base, apart=True)
                for j in range(J):
                    ins = dve.match_replace(taken[:, j, :], top[:, j, :], masked[:, j, :], -1.0)
                step(ins, base)
                dve.tensor_scalar(chosen[:], taken[:], 0.0, None, ALU.is_lt).then_inc(chosen_made, 1)
                step(dve.tensor_reduce(wsum[:], top[:], AX_X, ALU.add), base)
                step(dve.tensor_scalar(wsum[:], wsum[:], 1e-9, None, ALU.max), base)
                step(dve.reciprocal(wsum[:], wsum[:]), base)
                at_least(dve, w_stored, 16 * g.n)
                step(dve.scalar_tensor_tensor(out=weight[:], in0=taken[:], scalar=0.0, in1=masked[:],
                                              op0=ALU.is_lt, op1=ALU.mult), base)
                dve.scalar_tensor_tensor(out=weight[:], in0=weight[:], scalar=SCALE,
                                         in1=wsum[:].unsqueeze(2).to_broadcast([P, J, E]),
                                         op0=ALU.mult, op1=ALU.mult).then_inc(w_made, 1)
                step(dve.tensor_reduce(nchosen[:], chosen[:].rearrange("p j e -> p e j"), AX_X, ALU.add), base)

            def place(g, base):
                pos = ppos[:, 0:J * E].rearrange("p (j e) -> p j e", j=J)
                dve.wait_ge(pos_done, g.n + 1)
                dve.tensor_tensor(earlier[1 - g.b][:], earlier[g.b][:], nchosen[:], ALU.add)
                dve.scalar_tensor_tensor(out=masked[:], in0=pos, scalar=float(CAP), in1=chosen[:],
                                         op0=ALU.is_lt, op1=ALU.mult)
                step(dve.tensor_tensor(key[:], expert_base[:].unsqueeze(1).to_broadcast([P, J, E]), pos,
                                       ALU.subtract), base)
                step(dve.tensor_tensor(key[:], key[:], masked[:], ALU.mult), base, apart=True)
                for j in range(J):
                    ins = dve.max(key8[:, j, :], key[:, j, :])
                step(ins, base)
                at_least(dve, scattered[g.b], SCATTER * g.i)
                dve.tensor_scalar(slots[g.b][:], key8[:], -1.0, float(OUTSIDE), ALU.mult, ALU.add).then_inc(
                    slots_made, 1)

            def hidden(g, i, base):
                dve.wait_ge(tanh_done, IB * g.n + i + 1)
                step(dve.scalar_tensor_tensor(out=gate_a[:], in0=gate_t[:], scalar=1.0, in1=pmm[0],
                                              op0=ALU.add, op1=ALU.mult), base)
                dve.wait_ge(up_done, IB * g.n + i + 1)
                at_least(dve, hid_hi_made, IB * g.n + i)
                dve.scalar_tensor_tensor(out=hid[:], in0=gate_a[:], scalar=0.5, in1=pmm[1],
                                         op0=ALU.mult, op1=ALU.mult).then_inc(hid_made, 1)

            def hidden_lo(g, i):
                dve.wait_ge(hid_hi_made, IB * g.n + i + 1)
                dve.tensor_tensor(shid_lo[:, i, :], hid[:], shid_hi[:, i, :].bitcast(F32),
                                  ALU.subtract).then_inc(hid_lo_made, 1)

            def output(g, j):
                dve.wait_ge(out_done, J * g.n + j + 1)
                dve.wait_ge(residual_loaded[j // 2], 16 * (g.n + 1))
                tile = outs[j // 2][:, j % 2, :]
                dve.tensor_tensor(tile, pout[j % 2], tile, ALU.add).then_inc(out_free, 1)

            def group(g, base, last=False):
                nxt = g.next()
                if not last:
                    moments(nxt)
                features_lo(1 + g.n, 0, feat_hi, feat_lo)
                if not last:
                    deviations(nxt, base)
                features_lo(1 + g.n, 1, feat_hi, feat_lo)
                if not last:
                    normalise(nxt, base)
                features_lo(1 + g.n, 2, feat_hi, feat_lo)
                features_lo(1 + g.n, 3, feat_hi, feat_lo)
                if not last:
                    lo_half(nxt.n + 2, 0, xt_hi[nxt.b], xt_lo[nxt.b])
                hidden(g, 0, base)
                hidden_lo(g, 0)
                if not last:
                    lo_half(nxt.n + 2, 1, xt_hi[nxt.b], xt_lo[nxt.b])
                hidden(g, 1, base)
                hidden_lo(g, 1)
                if last:
                    gate_up_lo(turn(0))
                else:
                    rank_groups(nxt, base)
                output(g, 0)
                if not last:
                    choose(nxt, base)
                output(g, 1)
                output(g, 2)
                if last:
                    dve.wait_ge(slot_rows_turned, 1)
                    dve.tensor_copy(slot_cols[:], plog[:, 0:P]).then_inc(slot_cols_made, 1)
                else:
                    place(nxt, base)
                output(g, 3)

            def gate_up_lo(e):
                dve.wait_ge(egu_hi_made, e.n + 1)
                dve.tensor_tensor(egu_lo[e.b], raw[e.b][:, 0:GU], egu_hi[e.b].bitcast(F32),
                                  ALU.subtract).then_inc(egu_lo_made, 1)

            dve.memset(earlier[0][:], 0.0).then_inc(out_free, 2)
            moments(turn(0))
            dve.wait_ge(xis_turned, 1)
            dve.tensor_copy(ab[:], ppos[:, 0:HB]).then_inc(ab_made, 1)
            deviations(turn(0), 0)
            normalise(turn(0), 0)
            dve.wait_ge(ab_made, 1)
            step(dve.scalar_tensor_tensor(out=corr[:], in0=ab[:], scalar=-0.5, in1=ab[:], op0=ALU.mult,
                                          op1=ALU.mult))
            step(dve.tensor_copy(corr_r[:], corr[:]))
            dve.tensor_copy(corr3[:, :, 0], corr_r[:].bitcast(F32))
            dve.tensor_copy(corr3[:, :, 2], corr_r[:].bitcast(F32))
            dve.tensor_tensor(corr3[:, :, 1], corr[:], corr_r[:].bitcast(F32), ALU.subtract).then_inc(
                corr3_made, 1)
            dve.wait_ge(ab2_exp, 1)
            dve.tensor_scalar(ab2[:], ab2[:], 1.0 / H, None, ALU.mult).then_inc(ab2_made, 1)
            for half in range(2):
                lo_half(0, half, proj_hi, proj_lo, (ptr, pmm2)[half])
            for half in range(2):
                lo_half(1, half, xt_hi[0], xt_lo[0], (pout2, ptr)[half])
            dve.wait_ge(iw_norm_made, HB - 1)
            split_norm(iw_norm)
            dve.wait_ge(router_hi_made, 1)
            dve.tensor_tensor(router[:, :, E:], router_raw, router[:, :, 0:E].bitcast(F32),
                              ALU.subtract).then_inc(router_made, 1)
            for half in range(2):
                lo_half(2, half, xt_hi[1], xt_lo[1], (pout2, ptr)[half])
            dve.wait_ge(consts_made, 1)
            rank_groups(turn(0), 0)
            features_lo(0, 0, wt_hi, wt_lo, scale=ab2[:, 0:1])
            features_lo(0, 1, wt_hi, wt_lo, scale=ab2[:, 1:2])
            choose(turn(0), 0)
            features_lo(0, 2, wt_hi, wt_lo, scale=ab2[:, 2:3])
            place(turn(0), 0)
            features_lo(0, 3, wt_hi, wt_lo, scale=ab2[:, 3:4])
            dve.wait_ge(shared_hi_made, 1)
            dve.tensor_tensor(sgu_lo[:], raw[0][:, 0:GU], sgu_hi[:].bitcast(F32), ALU.subtract).then_inc(
                shared_lo_made, 1)
            dve.wait_ge(shared_hi_made, 2)
            dve.tensor_tensor(sdn_lo[:], raw[0][:, GU:], sdn_hi[:].bitcast(F32), ALU.subtract).then_inc(
                shared_lo_made, 1)

            start, per_group = steps[0], 36
            for n in range(2):
                steps[0] = 0
                group(turn(n), start + per_group * n)
            with dve.Fori(1, GROUPS // 2 - 1) as i:
                for b in range(2):
                    steps[0] = 0
                    group(Turn(i, b), start + per_group * (2 * i + b))
                    assert steps[0] == per_group, steps
            steps[0] = 0
            group(turn(GROUPS - 2), start + per_group * (GROUPS - 2))
            steps[0] = 0
            group(turn(GROUPS - 1), start + per_group * (GROUPS - 1), last=True)

            def down_lo(e):
                dve.wait_ge(edn_hi_made, e.n + 1)
                dve.tensor_tensor(edn_lo[e.b], raw[e.b][:, GU:], edn_hi[e.b].bitcast(F32),
                                  ALU.subtract).then_inc(edn_lo_made, 1)

            def e_turned_lo(e):
                dve.wait_ge(e_xt_hi_made, e.n + 1)
                dve.tensor_tensor(xt_lo[e.b][:, :, 0:CAP], ptr_e, xt_hi[e.b][:, :, 0:CAP].bitcast(F32),
                                  ALU.subtract).then_inc(e_xt_lo_made, 1)

            def slot_weights(e):
                at_least(dve, e_out_made, CB * (e.n - 1))
                dve.tensor_copy(slot_w[e.b][:].unsqueeze(2), xe[e.b][:, :, bass.ds(H + e.n, 1)]).then_inc(
                    slot_w_made, 1)

            def e_hidden(e):
                dve.wait_ge(silu_done, e.n + 1)
                dve.wait_ge(e_up_done, e.n + 1)
                at_least(dve, e_hid_hi_made, e.n)
                at_least(dve, e_hid_lo_made, e.n)
                dve.tensor_tensor(hid[:], gate_t[:], pmm[1], ALU.mult).then_inc(e_hid_made, 1)

            def e_hidden_lo(e):
                dve.wait_ge(e_hid_hi_made, e.n + 1)
                dve.tensor_tensor(hid_lo[:, e.b].rearrange("p a b -> p (a b)"), hid[:],
                                  hid_hi[:, e.b].rearrange("p a b -> p (a b)").bitcast(F32),
                                  ALU.subtract).then_inc(e_hid_lo_made, 1)

            def stage(e, turn_next=True):
                slot_weights(e)
                if turn_next:
                    e_turned_lo(e.next())
                    gate_up_lo(e.next())
                e_hidden(e)
                down_lo(e)
                e_hidden_lo(e)

            e_turned_lo(turn(0))
            stage(turn(0))
            stage(turn(1))
            with dve.Fori(1, E // 2 - 1) as i:
                for b in range(2):
                    stage(Turn(i, b))
            stage(turn(E - 2))
            stage(turn(E - 1), turn_next=False)

        @block.tensor
        def _(pe):
            def products(psum, pairs, first=True, final=True):
                for n, (lh, ll, rh, rl) in enumerate(pairs):
                    pe.matmul(psum, lh, rh, start=first and n == 0, stop=False)
                    pe.matmul(psum, lh, rl, start=False, stop=False)
                    ins = pe.matmul(psum, ll, rh, start=False, stop=final and n == len(pairs) - 1)
                return ins

            def turn_half(n, src, half, small=None, psum=ptr, free=None):
                at_least(pe, xt_lo_made, 2 * n + half if free is None else free)
                for h in range(2):
                    for j in range(J):
                        at = (2 * half + h) * P
                        ins = pe.transpose(psum[:, h, j * P:(j + 1) * P], src[:, j, at:at + P], ident[:])
                if small is not None:
                    for j in range(J):
                        ins = pe.transpose(ppos[0:3, j * P:(j + 1) * P], small[:, j, :], ident[:])
                ins.then_inc(turned, 1)

            def dots(s, r, hi, lo, row):
                at = slice(r * P, (r + 1) * P)
                products(pmm[r % 2], [(proj_hi[:, d, at], proj_lo[:, d, at], hi[:, d, :], lo[:, d, :])
                                         for d in range(HB)], final=False)
                pe.matmul(pmm[r % 2], corr_row[:, at], row[:], start=False, stop=True).then_inc(dot_done, 1)

            def dense_dots(g):
                pe.wait_ge(xt_lo_made, 2 * (g.n + 2) + 2)
                pe.wait_ge(norm_row_made, g.n + 2)
                for r in range(HB):
                    if r < 2:
                        at_least(pe, hid_made, IB * g.n)
                        pe.wait_ge(exp_done, HB * (g.n + 1) + r - 1)
                    else:
                        pe.wait_ge(exp_done, HB * (g.n + 1) + r - 1)
                    dots(1 + g.n, r, xt_hi[g.b], xt_lo[g.b], norm_row[g.b])

            def gate_up(g, i):
                for m, done in ((0, gate_done), (1, up_done)):
                    if i == 0:
                        pe.wait_ge(exp_done, HB * (g.n + 2) - 1 + m)
                    else:
                        pe.wait_ge(hid_made, IB * g.n + 1)
                    at = [slice(m * HB * I + h * I + i * P, m * HB * I + h * I + (i + 1) * P) for h in range(HB)]
                    products(pmm[m], [(sgu_hi[:, at[h]], sgu_lo[:, at[h]], xt_hi[g.b][:, h, :],
                                          xt_lo[g.b][:, h, :]) for h in range(HB)]).then_inc(done, 1)

            def logits(g):
                first = isinstance(g.n, int) and g.n == 0
                pe.wait_ge(xt_lo_made, 4 if first else 2 * (g.n + 2) + 2)
                at_least(pe, logit_made, g.n)
                for j in range(J):
                    at = slice(j * P, (j + 1) * P)
                    for h in range(HB):
                        for part in (xt_hi, xt_lo):
                            ins = pe.matmul(plog[:, at], part[g.b][:, h, at], router[:, h, :],
                                            start=(h == 0 and part is xt_hi),
                                            stop=(h == HB - 1 and part is xt_lo))
                ins.then_inc(logits_done, 1)

            def positions(g):
                pe.wait_ge(chosen_made, g.n + 1)
                pe.wait_ge(norm_row_made, g.n + 2)
                at_least(pe, slots_made, g.n)
                for j in range(J):
                    at = ppos[:, j * E:(j + 1) * E]
                    pe.matmul(at, before[:], chosen[:, j, :], start=True, stop=False)
                    for k in range(j):
                        pe.matmul(at, ones[:], chosen[:, k, :], start=False, stop=False)
                    ins = pe.matmul(at, ones[:], earlier[g.b][:], start=False, stop=True)
                ins.then_inc(pos_done, 1)

            def output(g, j):
                at = slice(j * P, (j + 1) * P)
                pe.wait_ge(feat_lo_made, HB * (g.n + 2))
                pe.wait_ge(hid_lo_made, IB * (g.n + 1))
                pe.wait_ge(out_free, J * g.n + j + 1)
                products(pout[j % 2], [(feat_hi[:, r, at], feat_lo[:, r, at], wt_hi[:, r, :], wt_lo[:, r, :])
                                          for r in range(HB)], final=False)
                products(pout[j % 2], [(shid_hi[:, i, at], shid_lo[:, i, at], sdn_hi[:, i * H:(i + 1) * H],
                                           sdn_lo[:, i * H:(i + 1) * H]) for i in range(IB)],
                         first=False).then_inc(out_done, 1)

            def group(g, last=False):
                nxt = g.next()
                dense_dots(g)
                if not last:
                    pe.wait_ge(xn_made, nxt.n + 1)
                    pe.wait_ge(norm3_made, nxt.n + 2)
                    turn_half(nxt.n + 2, xn, 0)
                gate_up(g, 0)
                if not last:
                    at_least(pe, slots_made, nxt.n)
                    turn_half(nxt.n + 2, xn, 1, norm3)
                gate_up(g, 1)
                if not last:
                    logits(nxt)
                output(g, 0)
                output(g, 1)
                output(g, 2)
                if last:
                    pe.wait_ge(slot_rows_loaded, 16)
                    pe.wait_ge(logit_made, GROUPS)
                    pe.transpose(plog[:, 0:P], slot_rows, ident[:]).then_inc(slot_rows_turned, 1)
                else:
                    positions(nxt)
                output(g, 3)

            pe.wait_ge(ident_made, 1)
            pe.wait_ge(xis_loaded, 16)
            pe.transpose(ppos[:, 0:HB], xis_row[:], ident[0:HB, 0:HB]).then_inc(xis_turned, 1)
            pe.wait_ge(proj_scaled, 1)
            turn_half(0, xbuf[1], 0, free=0)
            turn_half(0, xbuf[1], 1, psum=pmm2, free=0)
            pe.wait_ge(corr3_made, 1)
            for r in range(HB):
                ins = pe.transpose(ppos[0:3, r * P:(r + 1) * P], corr3[:, r, :], ident[:])
            ins.then_inc(corr_turned, 1)
            pe.wait_ge(xn_made, 1)
            turn_half(1, xn, 0, psum=pout2, free=0)
            pe.wait_ge(norm3_made, 1)
            pe.wait_ge(corr_row_made, 1)
            turn_half(1, xn, 1, norm3, free=1)
            turn_half(2, iw_raw, 0, psum=pout2, free=3)
            pe.wait_ge(norm3_made, 2)
            pe.wait_ge(norm_row_made, 1)
            turn_half(2, iw_raw, 1, norm3, free=4)
            pe.wait_ge(router_made, 1)
            logits(turn(0))
            pe.wait_ge(xt_lo_made, 6)
            pe.wait_ge(norm_row_made, 2)
            for r in range(HB):
                if r >= 2:
                    pe.wait_ge(exp_done, r - 1)
                dots(0, r, xt_hi[1], xt_lo[1], norm_row[1])
            pe.wait_ge(consts_made, 1)
            positions(turn(0))
            pe.wait_ge(shared_lo_made, 2)
            group(turn(0))
            group(turn(1))
            with pe.Fori(1, GROUPS // 2 - 1) as i:
                for b in range(2):
                    group(Turn(i, b))
            group(turn(GROUPS - 2))
            group(turn(GROUPS - 1), last=True)

            def e_turn(e):
                pe.wait_ge(gathered[e.b], 16 * CB * (e.i + 1))
                at_least(pe, e_xt_lo_made, e.n)
                for h in range(HB):
                    for c in range(CB):
                        ins = pe.transpose(ptr_e[:, h, c * P:(c + 1) * P], xe[e.b][:, c, h * P:(h + 1) * P],
                                           ident[:])
                ins.then_inc(e_turned, 1)

            def e_gate_up(e):
                pe.wait_ge(e_xt_lo_made, e.n + 1)
                pe.wait_ge(egu_lo_made, e.n + 1)
                at_least(pe, e_hid_made, e.n)
                for m, done in ((0, e_gate_done), (1, e_up_done)):
                    for i in range(IB):
                        at = [slice(m * HB * I + h * I + i * P, m * HB * I + h * I + (i + 1) * P)
                              for h in range(HB)]
                        ins = products(pmm[m][:, i * CAP:(i + 1) * CAP], [
                            (egu_hi[e.b][:, at[h]], egu_lo[e.b][:, at[h]], xt_hi[e.b][:, h, 0:CAP],
                             xt_lo[e.b][:, h, 0:CAP]) for h in range(HB)])
                    ins.then_inc(done, 1)

            def e_down(e):
                pe.wait_ge(e_hid_lo_made, e.n + 1)
                pe.wait_ge(edn_lo_made, e.n + 1)
                for c in range(CB):
                    at_least(pe, e_out_made, CB * (e.n - 1) + c + 1)
                    at = slice(c * P, (c + 1) * P)
                    products(pout[c], [
                        (hid_hi[:, e.b, i, at], hid_lo[:, e.b, i, at], edn_hi[e.b][:, i * H:(i + 1) * H],
                         edn_lo[e.b][:, i * H:(i + 1) * H]) for i in range(IB)]).then_inc(down_done, 1)

            e_turn(turn(0))
            e_turn(turn(1))
            e_gate_up(turn(0))
            pe.wait_ge(out_free, 2 + J * GROUPS)
            e_turn(turn(2))
            e_gate_up(turn(1))
            e_down(turn(0))
            with pe.Fori(1, E // 2 - 1) as i:
                for b in range(2):
                    e = Turn(i, b)
                    e_turn(e.next())
                    e_gate_up(e)
                    e_down(e.prev())
            e_turn(turn(E - 1))
            e_gate_up(turn(E - 2))
            e_down(turn(E - 3))
            e_gate_up(turn(E - 1))
            e_down(turn(E - 2))
            e_down(turn(E - 1))

        @block.gpsimd
        def _(pool):
            steps = [0]

            def step(ins):
                ins.then_inc(pool_step, 1)
                steps[0] += 1

            def wait_apart(sem, value):
                pool.wait_ge(sem, value)
                pool.tensor_tensor(pool_sink[:], pool_carrier[:], pool_carrier[:], ALU.add)

            step(pool.memset(ident[:], 0.0))
            pool.wait_ge(pool_step, steps[0])
            pool.affine_select(out=ident[:], in_=ident[:], compare_op=ALU.not_equal, fill=1.0, base=0,
                               pattern=[[-1, P]], channel_multiplier=1).then_inc(ident_made, 1)
            step(pool.memset(pool_carrier[:], 0.0))
            step(pool.memset(before[:], 1.0))
            step(pool.memset(ones[:], 1.0))
            step(pool.memset(lower[:], 1.0))
            step(pool.memset(zeros, 0.0))
            step(pool.iota(token_ids_i[:], [[P, GROUPS * J]], base=0, channel_multiplier=1))
            step(pool.iota(no_token_i, [[1, CAP]], base=TOKENS, channel_multiplier=0))
            step(pool.iota(expert_base_i[:], [[-CAP, E]], base=OUTSIDE, channel_multiplier=0))
            pool.wait_ge(pool_step, steps[0])
            step(pool.affine_select(out=before[:], in_=before[:], compare_op=ALU.is_gt, fill=0.0, base=0,
                                    pattern=[[1, P]], channel_multiplier=-1))
            step(pool.affine_select(out=lower[:], in_=lower[:], compare_op=ALU.is_gt, fill=0.0, base=0,
                                    pattern=[[1, RG], [-1, RG]], channel_multiplier=0))
            step(pool.tensor_copy(token_ids[:], token_ids_i[:]))
            step(pool.tensor_copy(no_token, no_token_i))
            pool.wait_ge(pool_step, steps[0])
            pool.tensor_copy(expert_base[:], expert_base_i[:]).then_inc(consts_made, 1)

            pool.wait_ge(table_made, 16 * (1 + 2 * SPARE // P))
            last_slot = pool.to_reg(SLOTS - 1)
            last_row = pool.to_reg(TOKENS + SPARE - 1)
            with pool.Fori(0, GROUPS // 2) as i:
                for b in range(2):
                    g = Turn(i, b)
                    pool.wait_ge(slots_made, g.n + 1)
                    pool.tensor_copy(ids[b][:], token_ids[:, bass.ds(J * g.n, J)]).then_inc(idx_copied, 1)
                    wait_apart(idx_copied, g.n + 1)
                    for j in range(J):
                        for k in range(K):
                            pool.indirect_dma_start(
                                out=slot_token, out_offset=bass.IndirectOffsetOnAxis(
                                    ap=slots[b][:, j, k:k + 1], axis=0),
                                in_=ids[b][:, j:j + 1], in_offset=None, bounds_check=last_slot,
                                oob_is_err=False).then_inc(scattered[b], 16)

            def gather(e, copied):
                pool.tensor_copy(gidx[e.b][:], slot_cols[:, bass.ds(CB * e.n, CB)]).then_inc(idx_copied, 1)
                wait_apart(idx_copied, copied)
                for c in range(CB):
                    pool.indirect_dma_start(
                        out=xe[e.b][:, c, :], out_offset=None, in_=rows,
                        in_offset=bass.IndirectOffsetOnAxis(ap=gidx[e.b][:, c:c + 1], axis=0),
                        bounds_check=last_row, oob_is_err=True).then_inc(gathered[e.b], 16)

            def add_rows(e, copied):
                at_least(pool, added, 16 * CB * e.n)
                pool.wait_ge(e_out_made, CB * (e.n + 1))
                pool.tensor_copy(sidx[e.b][:], slot_cols[:, bass.ds(CB * e.n, CB)]).then_inc(idx_copied, 1)
                wait_apart(idx_copied, copied)
                for c in range(CB):
                    pool.indirect_dma_start(
                        out=out, out_offset=bass.IndirectOffsetOnAxis(ap=sidx[e.b][:, c:c + 1], axis=0),
                        in_=outs[e.b][:, c, :], in_offset=None, bounds_check=last_row,
                        oob_is_err=True, compute_op=ALU.add).then_inc(added, 16)

            pool.wait_ge(slot_cols_made, 1)
            pool.wait_ge(xn_stored, 16 * GROUPS)
            pool.wait_ge(w_stored, 16 * GROUPS)
            gather(turn(0), GROUPS + 1)
            gather(turn(1), GROUPS + 2)
            pool.wait_ge(slot_w_made, 1)
            gather(turn(2), GROUPS + 3)
            for b in range(2):
                pool.wait_ge(out_stored[b], 16 * GROUPS)

            def stage(e):
                pool.wait_ge(slot_w_made, e.n + 1)
                gather(Turn(e.i + 1, e.b), GROUPS + 2 * e.n + 2)
                add_rows(e.prev(), GROUPS + 2 * e.n + 3)

            stage(turn(1))
            with pool.Fori(1, E // 2 - 1) as i:
                for b in range(2):
                    stage(Turn(i, b))
            for n in (E - 3, E - 2, E - 1):
                add_rows(turn(n), GROUPS + E + n + 1)
            pool.wait_ge(added, 16 * CB * E)


_INS = ['L0_attn_x', 'L0_attn_input_weights', 'L0_attn_xis', 'L0_attn_proj_matrix', 'L0_ffn_router_w',
        'L0_ffn_gate_w', 'L0_ffn_up_w', 'L0_ffn_down_w', 'L0_ffn_shared_gate_w', 'L0_ffn_shared_up_w',
        'L0_ffn_shared_down_w']


def kernel(**inputs):
    import numpy as _np
    import concourse.bacc as _bacc
    from concourse import mybir as _mybir
    from concourse.bass_utils import run_bass_kernel_spmd as _run

    nc = _bacc.Bacc("TRN2", target_bir_lowering=False, num_devices=1)
    arrays, args = {}, []
    for name in _INS:
        a = _np.ascontiguousarray(inputs[name])
        arrays[f"in_{name}_dram"] = a
        args.append(nc.dram_tensor(f"in_{name}_dram", a.shape, _mybir.dt.from_np(a.dtype), kind="ExternalInput").ap())
    args.append(nc.dram_tensor("out_0_dram", (TOKENS + SPARE, H), _mybir.dt.from_np(_np.dtype("float32")),
                               kind="ExternalOutput").ap())
    build(nc, *args)
    r = _run(nc, [arrays], core_ids=[0])
    return r.results[0]["out_0_dram"][:TOKENS].reshape(4, 2048, H)
```

```python
from contextlib import ExitStack

import concourse.bass as bass
from concourse import mybir

ALU = mybir.AluOpType
ACT = mybir.ActivationFunctionType
F32 = mybir.dt.float32
F32R = mybir.dt.float32r
BF16 = mybir.dt.bfloat16
I32 = mybir.dt.int32
U32 = mybir.dt.uint32
AX_X = mybir.AxisListType.X

P = 128
H = 512
HB = H // P
TOKENS = 8192
GROUP = 512
J = GROUP // P
GROUPS = TOKENS // GROUP
E = 64
EG = 8
RG = E // EG
TOP_GROUPS = 4
K = 8
CAP = 256
CB = CAP // P
I = 256
IB = I // P
SCALE = 2.5
EPS = 1e-5
RSQRT_SEED = 0x5F3759DF
SLOTS = E * CAP
SPARE = CAP
ROW = H + E
GU = 2 * HB * I
DN = IB * H
OUTSIDE = 2 * SLOTS
SCATTER = 16 * J * K


class Turn:

    def __init__(self, i, b, odd=0):
        self.i, self.b, self.odd = i, b, odd
        self.n = 2 * i + b
        self.q = 2 * odd + b

    def next(self):
        return Turn(self.i, 1, self.odd) if self.b == 0 else Turn(self.i + 1, 0, 1 - self.odd)

    def prev(self):
        return Turn(self.i, 0, self.odd) if self.b == 1 else Turn(self.i - 1, 1, 1 - self.odd)


def turn(n):
    return Turn(n // 2, n % 2, n // 2 % 2)


def four(i, k):
    return Turn(i + k // 2, k % 2, 1 - k // 2)


def at_least(eng, sem, value):
    if not (isinstance(value, int) and value <= 0):
        eng.wait_ge(sem, value)


def build(nc, x, iw, xis, proj, router_w, gate_w, up_w, down_w, sgate_w, sup_w, sdown_w, out):
    with ExitStack() as ctx:
        def sb(name, shape, dt=F32):
            return ctx.enter_context(nc.sbuf_tensor(name, shape, dt))

        def ps(name, shape):
            return ctx.enter_context(nc.psum_tensor(name, shape, F32))

        def sem(name):
            return ctx.enter_context(nc.semaphore(name))

        rows = nc.dram_tensor("rows", [TOKENS + SPARE, ROW], F32).ap()
        slot_token = nc.dram_tensor("slot_token", [SLOTS, 1], F32).ap()

        ident = sb("ident", [P, P])
        fold = sb("fold", [P, E])
        before = sb("before", [P, P], BF16)
        ones = sb("ones", [P, P], BF16)
        lower = sb("lower", [P, RG, RG])
        expert_base = sb("expert_base", [P, E])
        token_ids_i = sb("token_ids_i", [P, GROUPS * J], I32)
        token_ids = sb("token_ids", [P, GROUPS * J])
        expert_base_i = sb("expert_base_i", [P, E], I32)
        proj_hi = sb("proj_hi", [P, HB, H], F32R)
        proj_lo = sb("proj_lo", [P, HB, H], F32R)
        wt_hi = sb("wt_hi", [P, HB, H], F32R)
        wt_lo = sb("wt_lo", [P, HB, H], F32R)
        sgu_hi = sb("sgu_hi", [P, GU], F32R)
        sgu_lo = sb("sgu_lo", [P, GU], F32R)
        sdn_hi = sb("sdn_hi", [P, DN], F32R)
        sdn_lo = sb("sdn_lo", [P, DN], F32R)
        router = sb("router", [P, HB, 2 * E], F32R)
        xis_row = sb("xis_row", [HB, P])
        ab = sb("ab", [P, HB])
        ab2 = sb("ab2", [P, HB])
        corr = sb("corr", [P, HB])
        corr_r = sb("corr_r", [P, HB], F32R)
        corr3 = sb("corr3", [P, HB, 3])
        corr_row = sb("corr_row", [3, H], F32R)
        xbuf = [sb(f"xbuf{b}", [P, J, H]) for b in range(2)]
        xn = sb("xn", [P, J, H])
        xt_hi = [sb(f"xt_hi{b}", [P, HB, GROUP], F32R) for b in range(2)]
        xt_lo = [sb(f"xt_lo{b}", [P, HB, GROUP], F32R) for b in range(2)]
        wait_carrier = sb("wait_carrier", [P, 1])
        pool_carrier = sb("pool_carrier", [P, 1])
        pool_sink = sb("pool_sink", [P, 1])
        pool_sink2 = sb("pool_sink2", [P, 1])
        stats = sb("stats", [P, J, 6])
        mean_var = sb("mean_var", [P, J, 2])
        var_eps = sb("var_eps", [P, J])
        rstd = sb("rstd", [P, J])
        rstd2 = sb("rstd2", [P, J])
        norm = sb("norm", [P, J])
        norm_r = sb("norm_r", [P, J], F32R)
        iw_norm = sb("iw_norm", [P, HB])
        norm3 = sb("norm3", [P, J, 3])
        norm_row = [sb(f"norm_row{b}", [3, GROUP], F32R) for b in range(2)]
        feat = sb("feat", [P, 2, GROUP])
        feat_hi = sb("feat_hi", [P, HB, GROUP], F32R)
        feat_lo = sb("feat_lo", [P, HB, GROUP], F32R)
        gate_t = sb("gate_t", [P, GROUP])
        gate_a = sb("gate_a", [P, GROUP])
        hid = sb("hid", [P, GROUP])
        hid_hi = sb("hid_hi", [P, 2, IB, CAP], F32R)
        hid_lo = sb("hid_lo", [P, 2, IB, CAP], F32R)
        shid_hi = hid_hi[:].rearrange("p a b c -> p (a b c)").rearrange("p (i t) -> p i t", i=IB)
        shid_lo = hid_lo[:].rearrange("p a b c -> p (a b c)").rearrange("p (i t) -> p i t", i=IB)
        outs = [sb(f"outs{b}", [P, 2, H]) for b in range(2)]
        expn = sb("expn", [P, J, E])
        score = sb("score", [P, J, E])
        gmax = sb("gmax", [P, J, RG])
        beats = sb("beats", [P, J, RG, 2 * RG])
        logits_t = beats[:].rearrange("p j g o -> p (j g o)")
        rank = sb("rank", [P, J * RG])
        masked = sb("masked", [P, J, E])
        top = sb("top", [P, J, K])
        taken = sb("taken", [P, J, E])
        chosen = sb("chosen", [P, J, E], BF16)
        wsum = sb("wsum", [P, J])
        weight = sb("weight", [P, J, E])
        nchosen = sb("nchosen", [P, E])
        earlier = [sb(f"earlier{b}", [P, E], BF16) for b in range(2)]
        key = sb("key", [P, J, E])
        key8 = sb("key8", [P, J, K])
        slots = [sb(f"slots{b}", [P, J, K], U32) for b in range(2)]
        ids = [sb(f"ids{b}", [P, J]) for b in range(2)]
        raw = [sb(f"raw{b}", [P, GU + DN]) for b in range(2)]
        slot_rows = key[:].rearrange("p j e -> p (j e)")[:, 0:P]
        slot_cols = sb("slot_cols", [P, P], U32)
        gidx = [sb(f"gidx{b}", [P, CB], U32) for b in range(2)]
        sidx = [sb(f"sidx{b}", [P, CB], U32) for b in range(2)]
        slot_w = [sb(f"slot_w{q}", [P, CB]) for q in range(4)]
        router_raw = gate_a[:, 0:HB * E].rearrange("p (c e) -> p c e", c=HB)
        square = hid
        iw_raw = raw[1][:, 0:HB * H].rearrange("p (c d) -> p c d", c=HB)
        zeros = outs[0][:].rearrange("p a h -> p (a h)")[:, 0:ROW]
        no_token_i = outs[1][0:E, 0, 0:CAP].bitcast(I32)
        no_token = outs[1][0:E, 1, 0:CAP]
        xe = [xbuf[b][:].rearrange("p j h -> p (j h)")[:, 0:CB * ROW].rearrange("p (c h) -> p c h", c=CB)
              for b in range(2)]
        egu_hi = [proj_hi[:].rearrange("p a b -> p (a b)"), sgu_hi[:, :]]
        egu_lo = [proj_lo[:].rearrange("p a b -> p (a b)"), sgu_lo[:, :]]
        edn_hi = [sdn_hi[:, :], feat_hi[:, 0:IB, :].rearrange("p a b -> p (a b)")]
        edn_lo = [sdn_lo[:, :], feat_lo[:, 0:IB, :].rearrange("p a b -> p (a b)")]

        ptr = ps("ptr", [P, 2, 512])
        pmm2 = ps("pmm", [P, 2, 512])
        pout2 = ps("pout", [P, 2, 512])
        pmm = [pmm2[:, b, :] for b in range(2)]
        pout = [pout2[:, b, :] for b in range(2)]
        plog = ps("plog", [P, 512])
        ppos = ps("ppos", [P, 512])
        ptr_e = ptr[:].rearrange("p a b -> p (a b)").rearrange("p (h c) -> p h c", h=HB)

        ident_made = sem("ident_made")
        consts_made = sem("consts_made")
        ab_made = sem("ab_made")
        iw_norm_made = sem("iw_norm_made")
        iw_norm_turned = sem("iw_norm_turned")
        pool_step = sem("pool_step")
        xis_loaded = sem("xis_loaded")
        proj_loaded = [sem(f"proj_loaded{half}") for half in range(2)]
        iw_loaded = [sem(f"iw_loaded{half}") for half in range(2)]
        router_loaded = sem("router_loaded")
        table_made = sem("table_made")
        xis_turned = sem("xis_turned")
        corr3_made = sem("corr3_made")
        corr_turned = sem("corr_turned")
        corr_row_made = sem("corr_row_made")
        ab2_exp = sem("ab2_exp")
        ab2_made = sem("ab2_made")
        router_hi_made = sem("router_hi_made")
        router_made = sem("router_made")
        shared_hi_made = sem("shared_hi_made")
        shared_lo_made = sem("shared_lo_made")
        vec_step = sem("vec_step")
        x_loaded = [sem(f"x_loaded{b}") for b in range(2)]
        moments_made = sem("moments_made")
        xn_made = sem("xn_made")
        norm3_made = sem("norm3_made")
        xn_stored = sem("xn_stored")
        w_made = sem("w_made")
        w_stored = sem("w_stored")
        turned = sem("turned")
        xt_hi_made = sem("xt_hi_made")
        xt_lo_made = sem("xt_lo_made")
        norm_row_made = sem("norm_row_made")
        dot_done = sem("dot_done")
        exp_done = sem("exp_done")
        feat_hi_made = sem("feat_hi_made")
        feat_lo_made = sem("feat_lo_made")
        gate_done = sem("gate_done")
        up_done = sem("up_done")
        tanh_done = sem("tanh_done")
        hid_made = sem("hid_made")
        hid_hi_made = sem("hid_hi_made")
        hid_lo_made = sem("hid_lo_made")
        out_done = sem("out_done")
        residual_loaded = [sem(f"residual_loaded{b}") for b in range(2)]
        out_free = sem("out_free")
        out_stored = [sem(f"out_stored{b}") for b in range(2)]
        logits_done = sem("logits_done")
        logits_t_done = sem("logits_t_done")
        logits_t_made = sem("logits_t_made")
        expn_made = sem("expn_made")
        chosen_made = sem("chosen_made")
        pos_done = sem("pos_done")
        slots_made = sem("slots_made")
        scattered = [sem(f"scattered{b}") for b in range(2)]
        slot_rows_loaded = sem("slot_rows_loaded")
        slot_rows_turned = sem("slot_rows_turned")
        slot_cols_made = sem("slot_cols_made")
        gu_loaded = [sem(f"gu_loaded{b}") for b in range(2)]
        dn_loaded = [sem(f"dn_loaded{b}") for b in range(2)]
        idx_copied = sem("idx_copied")
        gathered = [sem(f"gathered{b}") for b in range(2)]
        slot_w_made = sem("slot_w_made")
        e_turned = sem("e_turned")
        e_xt_hi_made = sem("e_xt_hi_made")
        e_xt_lo_made = sem("e_xt_lo_made")
        egu_hi_made = sem("egu_hi_made")
        egu_lo_made = sem("egu_lo_made")
        edn_hi_made = sem("edn_hi_made")
        edn_lo_made = sem("edn_lo_made")
        e_gate_done = sem("e_gate_done")
        e_up_done = sem("e_up_done")
        silu_done = sem("silu_done")
        e_hid_made = sem("e_hid_made")
        e_hid_hi_made = sem("e_hid_hi_made")
        e_hid_lo_made = sem("e_hid_lo_made")
        down_done = sem("down_done")
        e_out_made = sem("e_out_made")
        added = sem("added")

        x_groups = x.rearrange("b s h -> (b s) h").rearrange("(g j p) h -> g p j h", j=J, p=P)
        x_halves = x.rearrange("b s h -> (b s) h").rearrange("(g a j p) h -> g a p j h", a=2, j=2, p=P)
        rows_groups = rows[0:TOKENS, :].rearrange("(g j p) h -> g p j h", j=J, p=P)
        out_halves = out[0:TOKENS, :].rearrange("(g a j p) h -> g a p j h", a=2, j=2, p=P)

        block = ctx.enter_context(nc.Block())

        @block.sync
        def _(sp):
            def load_x(g):
                sp.dma_start(xbuf[g.b][:], x_groups[g.n]).then_inc(x_loaded[g.b], 16)

            def load_gate_up(b, gate, up):
                sp.dma_start(raw[b][:, 0:GU // 2].rearrange("p (c i) -> p c i", c=HB),
                             gate.rearrange("(c p) i -> p c i", p=P)).then_inc(gu_loaded[b], 16)
                sp.dma_start(raw[b][:, GU // 2:GU].rearrange("p (c i) -> p c i", c=HB),
                             up.rearrange("(c p) i -> p c i", p=P)).then_inc(gu_loaded[b], 16)

            def load_down(b, down):
                sp.dma_start(raw[b][:, GU:].rearrange("p (c h) -> p c h", c=IB),
                             down.rearrange("(c p) h -> p c h", p=P)).then_inc(dn_loaded[b], 16)

            def store_xn(g):
                sp.wait_ge(xn_made, g.n + 1)
                sp.dma_start(rows_groups[g.n][:, :, 0:H], xn[:]).then_inc(xn_stored, 16)

            def store_w(g):
                sp.wait_ge(w_made, g.n + 1)
                sp.dma_start(rows_groups[g.n][:, :, H:ROW], weight[:]).then_inc(w_stored, 16)

            def load_residual(g):
                for a in range(2):
                    at_least(sp, out_stored[a], 16 * g.n)
                    sp.dma_start(outs[a][:], x_halves[g.n, a]).then_inc(residual_loaded[a], 16)

            def store_out(g, a):
                sp.wait_ge(out_free, 2 + J * g.n + 2 * a + 2)
                sp.dma_start(out_halves[g.n, a], outs[a][:]).then_inc(out_stored[a], 16)

            def group(g, load=True, last=False):
                load_residual(g)
                if load:
                    load_x(Turn(g.i + 1, g.b))
                if not last:
                    store_xn(g.next())
                store_out(g, 0)
                if not last:
                    store_w(g.next())
                store_out(g, 1)

            sp.dma_start(xis_row[:], xis.rearrange("(c p) -> c p", p=P)).then_inc(xis_loaded, 16)
            for source, place, loaded in ((proj, xbuf[1], proj_loaded), (iw, iw_raw, iw_loaded)):
                for half in range(2):
                    at = slice(half * H // 2, (half + 1) * H // 2)
                    sp.dma_start(place[:, :, at], source.rearrange("(c p) d -> p c d", p=P)[:, :, at]).then_inc(
                        loaded[half], 16)
            load_x(turn(0))
            sp.dma_start(router_raw, router_w.rearrange("(c p) e -> p c e", p=P)).then_inc(router_loaded, 16)
            load_gate_up(0, sgate_w, sup_w)
            load_down(0, sdown_w)
            sp.wait_ge(consts_made, 1)
            sp.dma_start(slot_token.rearrange("(e s) o -> e (s o)", s=CAP), no_token).then_inc(table_made, 16)
            for c in range(SPARE // P):
                at = slice(TOKENS + c * P, TOKENS + (c + 1) * P)
                sp.dma_start(rows[at, :], zeros).then_inc(table_made, 16)
                sp.dma_start(out[at, :], zeros[:, 0:H]).then_inc(table_made, 16)
            sp.wait_ge(turned, 2)
            load_x(turn(1))
            sp.wait_ge(iw_norm_turned, 1)
            load_gate_up(1, gate_w[1], up_w[1])
            load_down(1, down_w[1])
            store_xn(turn(0))
            sp.wait_ge(shared_lo_made, 2)
            load_gate_up(0, gate_w[0], up_w[0])
            load_down(0, down_w[0])
            sp.wait_ge(table_made, 16 * (1 + 2 * SPARE // P))
            store_w(turn(0))
            group(turn(0))
            group(turn(1))
            with sp.Fori(1, GROUPS // 2 - 1) as i:
                for b in range(2):
                    group(Turn(i, b))
            group(turn(GROUPS - 2), load=False)
            load_residual(turn(GROUPS - 1))
            for b in range(2):
                sp.wait_ge(scattered[b], SCATTER * GROUPS // 2)
            sp.dma_start(slot_rows, slot_token.rearrange("(q p) o -> q (p o)", p=P)).then_inc(
                slot_rows_loaded, 16)
            store_out(turn(GROUPS - 1), 0)
            sp.wait_ge(egu_lo_made, 1)
            load_gate_up(0, gate_w[2], up_w[2])
            store_out(turn(GROUPS - 1), 1)

            def refill(e):
                b = e.b
                sp.wait_ge(egu_hi_made, e.n - 1)
                sp.wait_ge(egu_lo_made, e.n - 1)
                load_gate_up(b, gate_w[e.n], up_w[e.n])
                sp.wait_ge(edn_hi_made, e.n - 1)
                sp.wait_ge(edn_lo_made, e.n - 1)
                load_down(b, down_w[e.n])

            sp.wait_ge(edn_lo_made, 1)
            load_down(0, down_w[2])
            refill(turn(3))
            with sp.Fori(2, E // 2) as i:
                for b in range(2):
                    refill(Turn(i, b))

        @block.scalar
        def _(act):
            copy = ACT.Copy

            def features(s, r, hi, scale=None):
                act.wait_ge(dot_done, HB * s + r + 1)
                at_least(act, feat_lo_made, HB * s + r - 1)
                act.activation(feat[:, r % 2], pmm[r % 2], ACT.Exp, scale=ab[:, r:r + 1]).then_inc(exp_done, 1)
                act.wait_ge(exp_done, HB * s + r + 1)
                if scale is None:
                    act.activation(hi[:, r, :], feat[:, r % 2], copy).then_inc(feat_hi_made, 1)
                else:
                    act.activation(hi[:, r, :], feat[:, r % 2], copy, scale=scale).then_inc(feat_hi_made, 1)

            def hidden(g, i):
                act.wait_ge(gate_done, IB * g.n + i + 1)
                at_least(act, hid_made, IB * g.n + i)
                act.activation(gate_t[:], pmm[0], ACT.Tanh, scale=0.5).then_inc(tanh_done, 1)

            def hidden_hi(g, i):
                act.wait_ge(hid_made, IB * g.n + i + 1)
                act.activation(shid_hi[:, i, :], hid[:], copy).then_inc(hid_hi_made, 1)

            def copy_logits(g):
                act.wait_ge(logits_t_done, g.n + 1)
                at_least(act, chosen_made, g.n)
                act.activation(logits_t, plog[:], copy).then_inc(logits_t_made, 1)

            def exp_logits(g):
                act.wait_ge(logits_done, g.n + 1)
                act.activation(expn[:].rearrange("p j e -> p (j e)"), plog[:, 0:J * E], ACT.Exp,
                               scale=-1.0).then_inc(expn_made, 1)

            def hi_half(n, half, dst, psum=ptr):
                act.wait_ge(turned, 2 * n + half + 1)
                act.activation(dst[:, 2 * half:2 * half + 2, :], psum[:], copy).then_inc(xt_hi_made, 1)

            def hi_norm(g):
                act.activation(norm_row[g.b][:], ppos[0:3, :], copy).then_inc(norm_row_made, 1)

            def group(g, last=False):
                nxt = g.next()
                for r in range(HB):
                    features(1 + g.n, r, feat_hi)
                if not last:
                    hi_half(nxt.n + 2, 0, xt_hi[nxt.b])
                hidden(g, 0)
                if not last:
                    hi_half(nxt.n + 2, 1, xt_hi[nxt.b])
                    hi_norm(nxt)
                hidden_hi(g, 0)
                if not last:
                    copy_logits(nxt)
                if not last:
                    exp_logits(nxt)
                hidden(g, 1)
                hidden_hi(g, 1)

            act.wait_ge(ab_made, 1)
            act.activation(ab2[:], ab[:], ACT.Exp, scale=2.0).then_inc(ab2_exp, 1)

            def square_sum(r):
                ins = act.activation(square[:] if r % 2 == 0 else gate_t[:], iw_raw[:, r, :], ACT.Square,
                                     accum_out=iw_norm[:, r:r + 1])
                if r >= 1:
                    ins.then_inc(iw_norm_made, 1)
                    act.wait_ge(iw_norm_made, r)

            hi_half(0, 0, proj_hi, ptr)
            hi_half(0, 1, proj_hi, pmm2)
            for half in range(2):
                hi_half(1, half, xt_hi[1], (pout2, ptr)[half])
            for half in range(2):
                act.wait_ge(iw_loaded[half], 16)
            for r in range(HB):
                square_sum(r)
            act.wait_ge(corr_turned, 1)
            act.activation(corr_row[:], ppos[0:3, :], copy).then_inc(corr_row_made, 1)
            act.wait_ge(iw_norm_turned, 1)
            hi_norm(turn(1))
            act.wait_ge(router_loaded, 16)
            act.activation(router[:, :, 0:E], router_raw, copy).then_inc(router_hi_made, 1)
            act.wait_ge(ab2_made, 1)
            features(0, 0, wt_hi, scale=ab2[:, 0:1])
            act.wait_ge(gu_loaded[0], 32)
            act.activation(sgu_hi[:], raw[0][:, 0:GU], copy).then_inc(shared_hi_made, 1)
            features(0, 1, wt_hi, scale=ab2[:, 1:2])
            features(0, 2, wt_hi, scale=ab2[:, 2:3])
            for half in range(2):
                hi_half(2, half, xt_hi[0], (pout2, ptr)[half])
            hi_norm(turn(0))
            features(0, 3, wt_hi, scale=ab2[:, 3:4])
            copy_logits(turn(0))
            exp_logits(turn(0))
            act.wait_ge(dn_loaded[0], 16)
            act.activation(sdn_hi[:], raw[0][:, GU:], copy).then_inc(shared_hi_made, 1)
            group(turn(0))
            group(turn(1))
            with act.Fori(1, GROUPS // 2 - 1) as i:
                for b in range(2):
                    group(Turn(i, b))
            group(turn(GROUPS - 2))
            group(turn(GROUPS - 1), last=True)

            def gate_up_hi(e):
                act.wait_ge(gu_loaded[e.b], 32 * (e.i + (2 if e.b == 0 else 1)))
                act.activation(egu_hi[e.b], raw[e.b][:, 0:GU], copy).then_inc(egu_hi_made, 1)

            def down_hi(e):
                act.wait_ge(dn_loaded[e.b], 16 * (e.i + (2 if e.b == 0 else 1)))
                act.activation(edn_hi[e.b], raw[e.b][:, GU:], copy).then_inc(edn_hi_made, 1)

            def e_turned_hi(e):
                act.wait_ge(e_turned, e.n + 1)
                act.activation(xt_hi[e.b][:, :, 0:CAP], ptr_e, copy).then_inc(e_xt_hi_made, 1)

            def e_silu(e):
                act.wait_ge(e_gate_done, e.n + 1)
                at_least(act, e_hid_made, e.n)
                act.activation(gate_t[:], pmm[0], ACT.Silu).then_inc(silu_done, 1)

            def e_hidden_hi(e):
                act.wait_ge(e_hid_made, e.n + 1)
                act.activation(hid_hi[:, e.b].rearrange("p a b -> p (a b)"), hid[:], copy).then_inc(
                    e_hid_hi_made, 1)

            def e_out(e):
                act.wait_ge(slot_w_made, e.n + 1)
                at_least(act, added, 16 * CB * (e.n - 1))
                for c in range(CB):
                    act.wait_ge(down_done, CB * e.n + c + 1)
                    act.activation(outs[e.b][:, c], pout[c], copy, scale=slot_w[e.q][:, c:c + 1]).then_inc(
                        e_out_made, 1)

            def stage(e, next_rows=True, next_weights=True, out_prev=True):
                if next_rows:
                    e_turned_hi(e.next())
                if next_weights:
                    gate_up_hi(e.next())
                e_silu(e)
                down_hi(e)
                e_hidden_hi(e)
                if out_prev:
                    e_out(e.prev())

            act.wait_ge(dot_done, HB * (GROUPS + 1))
            gate_up_hi(turn(0))
            act.wait_ge(up_done, IB * GROUPS)
            gate_up_hi(turn(1))
            e_turned_hi(turn(0))
            stage(turn(0), next_weights=False, out_prev=False)
            for b in range(2):
                act.wait_ge(out_stored[b], 16 * GROUPS)
            stage(turn(1))
            with act.Fori(1, E // 2 - 2, 2) as i:
                for k in range(4):
                    stage(four(i, k))
            stage(turn(E - 2))
            stage(turn(E - 1), next_rows=False, next_weights=False)
            e_out(turn(E - 1))

        @block.vector
        def _(dve):
            steps = [0]

            def step(ins, base=0, apart=False):
                ins.then_inc(vec_step, 1)
                steps[0] += 1
                dve.wait_ge(vec_step, base + steps[0])
                if apart:
                    dve.memset(wait_carrier[:], 0.0)

            def split_norm(norm, base=0):
                step(dve.tensor_copy(norm_r[:], norm[:]), base)
                dve.tensor_copy(norm3[:, :, 0:2], norm_r[:].bitcast(F32).unsqueeze(2).to_broadcast([P, J, 2]))
                dve.tensor_tensor(norm3[:, :, 2], norm[:], norm_r[:].bitcast(F32), ALU.subtract).then_inc(
                    norm3_made, 1)

            def lo_half(n, half, hi, lo, psum=ptr):
                dve.wait_ge(xt_hi_made, 2 * n + half + 1)
                at = slice(2 * half, 2 * half + 2)
                dve.tensor_tensor(lo[:, at, :], psum[:], hi[:, at, :].bitcast(F32), ALU.subtract).then_inc(
                    xt_lo_made, 1)

            def features_lo(s, r, hi, lo, scale=1.0):
                dve.wait_ge(feat_hi_made, HB * s + r + 1)
                if isinstance(scale, float):
                    ins = dve.tensor_tensor(lo[:, r, :], feat[:, r % 2], hi[:, r, :].bitcast(F32), ALU.subtract)
                else:
                    ins = dve.scalar_tensor_tensor(out=lo[:, r, :], in0=feat[:, r % 2], scalar=scale,
                                                   in1=hi[:, r, :].bitcast(F32), op0=ALU.mult,
                                                   op1=ALU.subtract)
                ins.then_inc(feat_lo_made, 1)

            def moments(g):
                dve.wait_ge(x_loaded[g.b], 16 * (g.i + 1))
                for j in range(J):
                    ins = dve.bn_stats(stats[:, j, :], xbuf[g.b][:, j, :])
                ins.then_inc(moments_made, 1)

            def deviations(g, base):
                dve.wait_ge(moments_made, g.n + 1)
                dve.memset(wait_carrier[:], 0.0)
                for j in range(J):
                    ins = dve.bn_aggr(mean_var[:, j, :], stats[:, j, :])
                step(ins, base)
                step(dve.tensor_scalar(var_eps[:], mean_var[:, :, 1], EPS, None, ALU.add), base)
                step(dve.tensor_scalar(rstd2[:].bitcast(I32), var_eps[:].bitcast(I32), 1, None,
                                       ALU.arith_shift_right), base)
                step(dve.tensor_scalar(rstd[:].bitcast(I32), rstd2[:].bitcast(I32), -1.0,
                                       float(RSQRT_SEED), ALU.mult, ALU.add), base)
                for _ in range(3):
                    step(dve.tensor_tensor(rstd2[:], rstd[:], rstd[:], ALU.mult), base)
                    step(dve.scalar_tensor_tensor(out=rstd2[:], in0=rstd2[:], scalar=-0.5, in1=var_eps[:],
                                                  op0=ALU.mult, op1=ALU.mult), base)
                    step(dve.scalar_tensor_tensor(out=rstd[:], in0=rstd2[:], scalar=1.5, in1=rstd[:],
                                                  op0=ALU.add, op1=ALU.mult), base)

            def normalise(g, base):
                dve.wait_ge(turned, 2 * (g.n + 2))
                at_least(dve, xn_stored, 16 * g.n)
                for j in range(J):
                    ins = dve.tensor_scalar(xn[:, j, :], xbuf[g.b][:, j, :], mean_var[:, j, 0:1],
                                            rstd[:, j:j + 1], ALU.subtract, ALU.mult)
                ins.then_inc(xn_made, 1)
                step(dve.tensor_tensor(rstd2[:], rstd[:], rstd[:], ALU.mult), base)
                step(dve.scalar_tensor_tensor(out=norm[:], in0=mean_var[:, :, 1], scalar=float(H),
                                              in1=rstd2[:], op0=ALU.mult, op1=ALU.mult), base)
                split_norm(norm, base)

            def scores(g, base):
                dve.wait_ge(expn_made, g.n + 1)
                step(dve.tensor_scalar(expn[:], expn[:], 1.0, None, ALU.add), base)
                step(dve.reciprocal(score[:], expn[:]), base)

            def best_in_group(base):
                step(dve.tensor_reduce(gmax[:], score[:].rearrange("p j (g e) -> p (j g) e", e=EG), AX_X,
                                       ALU.max), base)

            def rank_groups(base):
                other = gmax[:].unsqueeze(2).to_broadcast([P, J, RG, RG])
                own = gmax[:].unsqueeze(3).to_broadcast([P, J, RG, RG])
                dve.tensor_tensor(beats[:, :, :, 0:RG], other, own, ALU.is_gt)
                step(dve.tensor_tensor(beats[:, :, :, RG:], other, own, ALU.is_equal), base)
                step(dve.tensor_tensor(beats[:, :, :, RG:], beats[:, :, :, RG:],
                                       lower[:].unsqueeze(1).to_broadcast([P, J, RG, RG]), ALU.mult), base)
                step(dve.tensor_reduce(rank[:], beats[:].rearrange("p j g o -> p (j g) o"), AX_X, ALU.add),
                     base)

            def choose(g, base):
                step(dve.scalar_tensor_tensor(
                    out=masked[:].rearrange("p j (g e) -> p (j g) e", e=EG),
                    in0=rank[:].unsqueeze(2).to_broadcast([P, J * RG, EG]), scalar=float(TOP_GROUPS),
                    in1=score[:].rearrange("p j (g e) -> p (j g) e", e=EG), op0=ALU.is_lt, op1=ALU.mult), base,
                    apart=True)
                for j in range(J):
                    ins = dve.max(top[:, j, :], masked[:, j, :])
                step(ins, base, apart=True)
                for j in range(J):
                    ins = dve.match_replace(taken[:, j, :], top[:, j, :], masked[:, j, :], -1.0)
                step(ins, base)
                dve.tensor_scalar(chosen[:], taken[:], 0.0, None, ALU.is_lt).then_inc(chosen_made, 1)

            def weigh(g, base):
                step(dve.tensor_reduce(wsum[:], top[:], AX_X, ALU.add), base)
                step(dve.tensor_scalar(wsum[:], wsum[:], 1e-9, None, ALU.max), base)
                step(dve.reciprocal(wsum[:], wsum[:]), base)
                at_least(dve, w_stored, 16 * g.n)
                step(dve.scalar_tensor_tensor(out=weight[:], in0=taken[:], scalar=0.0, in1=masked[:],
                                              op0=ALU.is_lt, op1=ALU.mult), base)
                dve.scalar_tensor_tensor(out=weight[:], in0=weight[:], scalar=SCALE,
                                         in1=wsum[:].unsqueeze(2).to_broadcast([P, J, E]),
                                         op0=ALU.mult, op1=ALU.mult).then_inc(w_made, 1)
                step(dve.tensor_reduce(nchosen[:], chosen[:].rearrange("p j e -> p e j"), AX_X, ALU.add), base)

            def place(g, base, psum=ppos[:, 0:J * E]):
                pos = psum.rearrange("p (j e) -> p j e", j=J)
                dve.wait_ge(pos_done, g.n + 1)
                dve.tensor_tensor(earlier[1 - g.b][:], earlier[g.b][:], nchosen[:], ALU.add)
                dve.scalar_tensor_tensor(out=masked[:], in0=pos, scalar=float(CAP), in1=chosen[:],
                                         op0=ALU.is_lt, op1=ALU.mult)
                step(dve.tensor_tensor(key[:], expert_base[:].unsqueeze(1).to_broadcast([P, J, E]), pos,
                                       ALU.subtract), base)
                step(dve.tensor_tensor(key[:], key[:], masked[:], ALU.mult), base, apart=True)
                for j in range(J):
                    ins = dve.max(key8[:, j, :], key[:, j, :])
                step(ins, base)
                at_least(dve, scattered[g.b], SCATTER * g.i)
                dve.tensor_scalar(slots[g.b][:], key8[:], -1.0, float(OUTSIDE), ALU.mult, ALU.add).then_inc(
                    slots_made, 1)

            def hidden(g, i, base):
                dve.wait_ge(tanh_done, IB * g.n + i + 1)
                step(dve.scalar_tensor_tensor(out=gate_a[:], in0=gate_t[:], scalar=1.0, in1=pmm[0],
                                              op0=ALU.add, op1=ALU.mult), base)
                dve.wait_ge(up_done, IB * g.n + i + 1)
                at_least(dve, hid_hi_made, IB * g.n + i)
                dve.scalar_tensor_tensor(out=hid[:], in0=gate_a[:], scalar=0.5, in1=pmm[1],
                                         op0=ALU.mult, op1=ALU.mult).then_inc(hid_made, 1)

            def hidden_lo(g, i):
                dve.wait_ge(hid_hi_made, IB * g.n + i + 1)
                dve.tensor_tensor(shid_lo[:, i, :], hid[:], shid_hi[:, i, :].bitcast(F32),
                                  ALU.subtract).then_inc(hid_lo_made, 1)

            def output(g, j):
                dve.wait_ge(out_done, J * g.n + j + 1)
                dve.wait_ge(residual_loaded[j // 2], 16 * (g.n + 1))
                tile = outs[j // 2][:, j % 2, :]
                dve.tensor_tensor(tile, pout[j % 2], tile, ALU.add).then_inc(out_free, 1)

            def group(g, base, before_last=False, last=False):
                nxt = g.next()
                features_lo(1 + g.n, 0, feat_hi, feat_lo)
                if not last:
                    deviations(nxt, base)
                features_lo(1 + g.n, 1, feat_hi, feat_lo)
                if not last:
                    normalise(nxt, base)
                features_lo(1 + g.n, 2, feat_hi, feat_lo)
                features_lo(1 + g.n, 3, feat_hi, feat_lo)
                if not last:
                    lo_half(nxt.n + 2, 0, xt_hi[nxt.b], xt_lo[nxt.b])
                    lo_half(nxt.n + 2, 1, xt_hi[nxt.b], xt_lo[nxt.b])
                hidden(g, 0, base)
                hidden_lo(g, 0)
                outputs(g, base, before_last, last)

            def outputs(g, base, before_last=False, last=False):
                nxt = g.next()
                if not last:
                    scores(nxt, base)
                    best_in_group(base)
                    rank_groups(base)
                hidden(g, 1, base)
                if not last:
                    choose(nxt, base)
                hidden_lo(g, 1)
                if not last:
                    weigh(nxt, base)
                output(g, 0)
                if not last:
                    place(nxt, base)
                output(g, 1)
                if last:
                    gate_up_lo(turn(0))
                    dve.wait_ge(slot_rows_turned, 1)
                    dve.tensor_copy(slot_cols[:], plog[:, 0:P]).then_inc(slot_cols_made, 1)
                elif not before_last:
                    moments(Turn(g.i + 1, g.b))
                output(g, 2)
                if last:
                    gate_up_lo(turn(1))
                else:
                    output(g, 3)

            def gate_up_lo(e):
                dve.wait_ge(egu_hi_made, e.n + 1)
                dve.tensor_tensor(egu_lo[e.b], raw[e.b][:, 0:GU], egu_hi[e.b].bitcast(F32),
                                  ALU.subtract).then_inc(egu_lo_made, 1)

            dve.memset(earlier[0][:], 0.0).then_inc(out_free, 2)
            dve.wait_ge(xis_turned, 1)
            dve.tensor_copy(ab[:], ppos[:, 0:HB]).then_inc(ab_made, 1)
            dve.wait_ge(ab_made, 1)
            step(dve.tensor_scalar(corr[:], ab[:], -0.5, None, ALU.mult))
            step(dve.tensor_copy(corr_r[:], corr[:]))
            dve.tensor_copy(corr3[:, :, 0], corr_r[:].bitcast(F32))
            dve.tensor_copy(corr3[:, :, 2], corr_r[:].bitcast(F32))
            dve.tensor_tensor(corr3[:, :, 1], corr[:], corr_r[:].bitcast(F32), ALU.subtract).then_inc(
                corr3_made, 1)
            dve.wait_ge(ab2_exp, 1)
            dve.tensor_scalar(ab2[:], ab2[:], 1.0 / H, None, ALU.mult).then_inc(ab2_made, 1)
            for half in range(2):
                lo_half(0, half, proj_hi, proj_lo, (ptr, pmm2)[half])
            for half in range(2):
                lo_half(1, half, xt_hi[1], xt_lo[1], (pout2, ptr)[half])
            dve.wait_ge(iw_norm_made, HB - 1)
            split_norm(iw_norm)
            moments(turn(0))
            deviations(turn(0), 0)
            dve.wait_ge(iw_norm_turned, 1)
            normalise(turn(0), 0)
            dve.wait_ge(ab2_made, 1)
            features_lo(0, 0, wt_hi, wt_lo, scale=ab2[:, 0:1])
            features_lo(0, 1, wt_hi, wt_lo, scale=ab2[:, 1:2])
            dve.wait_ge(router_hi_made, 1)
            dve.tensor_tensor(router[:, :, E:], router_raw, router[:, :, 0:E].bitcast(F32),
                              ALU.subtract).then_inc(router_made, 1)
            features_lo(0, 2, wt_hi, wt_lo, scale=ab2[:, 2:3])
            for half in range(2):
                lo_half(2, half, xt_hi[0], xt_lo[0], (pout2, ptr)[half])
            features_lo(0, 3, wt_hi, wt_lo, scale=ab2[:, 3:4])
            moments(turn(1))
            deviations(turn(1), 0)
            dve.wait_ge(consts_made, 1)
            scores(turn(0), 0)

            def first_group(g, base):
                nxt = g.next()
                features_lo(1, 0, feat_hi, feat_lo)
                normalise(nxt, base)
                features_lo(1, 1, feat_hi, feat_lo)
                best_in_group(base)
                rank_groups(base)
                features_lo(1, 2, feat_hi, feat_lo)
                features_lo(1, 3, feat_hi, feat_lo)
                lo_half(nxt.n + 2, 0, xt_hi[nxt.b], xt_lo[nxt.b])
                choose(g, base)
                weigh(g, base)
                lo_half(nxt.n + 2, 1, xt_hi[nxt.b], xt_lo[nxt.b])
                hidden(g, 0, base)
                hidden_lo(g, 0)
                place(g, base, pout[1][:, 0:J * E])
                outputs(g, base)

            start, per_group = steps[0], 35
            steps[0] = 0
            first_group(turn(0), start)
            start += steps[0] - per_group
            steps[0] = 0
            group(turn(1), start + per_group)
            with dve.Fori(1, GROUPS // 2 - 1) as i:
                for b in range(2):
                    steps[0] = 0
                    group(Turn(i, b), start + per_group * (2 * i + b))
                    assert steps[0] == per_group, steps
            steps[0] = 0
            group(turn(GROUPS - 2), start + per_group * (GROUPS - 2), before_last=True)
            steps[0] = 0
            group(turn(GROUPS - 1), start + per_group * (GROUPS - 1), last=True)

            def down_lo(e):
                dve.wait_ge(edn_hi_made, e.n + 1)
                dve.tensor_tensor(edn_lo[e.b], raw[e.b][:, GU:], edn_hi[e.b].bitcast(F32),
                                  ALU.subtract).then_inc(edn_lo_made, 1)

            def slot_weights(e):
                at_least(dve, e_out_made, CB * (e.n - 3))
                dve.tensor_copy(slot_w[e.q][:].unsqueeze(2), xe[e.b][:, :, bass.ds(H + e.n, 1)]).then_inc(
                    slot_w_made, 1)

            def e_turned_lo(e):
                dve.wait_ge(e_xt_hi_made, e.n + 1)
                slot_weights(e)
                dve.tensor_tensor(xt_lo[e.b][:, :, 0:CAP], ptr_e, xt_hi[e.b][:, :, 0:CAP].bitcast(F32),
                                  ALU.subtract).then_inc(e_xt_lo_made, 1)

            def e_hidden(e):
                dve.wait_ge(silu_done, e.n + 1)
                dve.wait_ge(e_up_done, e.n + 1)
                at_least(dve, e_hid_hi_made, e.n)
                at_least(dve, e_hid_lo_made, e.n)
                dve.tensor_tensor(hid[:], gate_t[:], pmm[1], ALU.mult).then_inc(e_hid_made, 1)

            def e_hidden_lo(e):
                dve.wait_ge(e_hid_hi_made, e.n + 1)
                dve.tensor_tensor(hid_lo[:, e.b].rearrange("p a b -> p (a b)"), hid[:],
                                  hid_hi[:, e.b].rearrange("p a b -> p (a b)").bitcast(F32),
                                  ALU.subtract).then_inc(e_hid_lo_made, 1)

            def stage(e, next_rows=True, next_weights=True):
                if next_rows:
                    e_turned_lo(e.next())
                if next_weights:
                    gate_up_lo(e.next())
                e_hidden(e)
                down_lo(e)
                e_hidden_lo(e)

            e_turned_lo(turn(0))
            output(turn(GROUPS - 1), 3)
            stage(turn(0), next_weights=False)
            stage(turn(1))
            with dve.Fori(1, E // 2 - 2, 2) as i:
                for k in range(4):
                    stage(four(i, k))
            stage(turn(E - 2))
            stage(turn(E - 1), next_rows=False, next_weights=False)

        @block.tensor
        def _(pe):
            def products(psum, pairs, first=True, final=True):
                for n, (lh, ll, rh, rl) in enumerate(pairs):
                    pe.matmul(psum, lh, rh, start=first and n == 0, stop=False)
                    pe.matmul(psum, lh, rl, start=False, stop=False)
                    ins = pe.matmul(psum, ll, rh, start=False, stop=final and n == len(pairs) - 1)
                return ins

            def turn_half(n, src, half, small=None, psum=ptr, free=None):
                at_least(pe, xt_lo_made, 2 * n + half if free is None else free)
                for h in range(2):
                    for j in range(J):
                        at = (2 * half + h) * P
                        ins = pe.transpose(psum[:, h, j * P:(j + 1) * P], src[:, j, at:at + P], ident[:])
                if small is not None:
                    ins = turn_small(small)
                ins.then_inc(turned, 1)

            def turn_small(small):
                for j in range(J):
                    ins = pe.transpose(ppos[0:3, j * P:(j + 1) * P], small[:, j, :], ident[:])
                return ins

            def dots(s, r, hi, lo, row):
                projected(r, hi, lo)
                less_norm(r, row)

            def projected(r, hi, lo, blocks=range(HB)):
                at = slice(r * P, (r + 1) * P)
                products(pmm[r % 2], [(proj_hi[:, d, at], proj_lo[:, d, at], hi[:, d, :], lo[:, d, :])
                                         for d in blocks], first=0 in blocks, final=False)

            def less_norm(r, row):
                pe.matmul(pmm[r % 2], corr_row[:, r * P:(r + 1) * P], row[:], start=False,
                          stop=True).then_inc(dot_done, 1)

            def dense_dots(g, blocks=range(HB)):
                pe.wait_ge(xt_lo_made, 2 * (g.n + 2) + 2)
                pe.wait_ge(norm_row_made, g.n + 2)
                for r in blocks:
                    if r < 2:
                        at_least(pe, hid_made, IB * g.n)
                    pe.wait_ge(exp_done, HB * (g.n + 1) + r - 1)
                    dots(1 + g.n, r, xt_hi[g.b], xt_lo[g.b], norm_row[g.b])

            def shared_products(g, i, m, blocks=range(HB)):
                if 0 in blocks and i == 0:
                    pe.wait_ge(exp_done, HB * (g.n + 2) - 1 + m)
                elif 0 in blocks:
                    pe.wait_ge(hid_made, IB * g.n + 1)
                final = HB - 1 in blocks
                at = [slice(m * HB * I + h * I + i * P, m * HB * I + h * I + (i + 1) * P) for h in range(HB)]
                ins = products(pmm[m], [(sgu_hi[:, at[h]], sgu_lo[:, at[h]], xt_hi[g.b][:, h, :],
                                         xt_lo[g.b][:, h, :]) for h in blocks],
                               first=0 in blocks, final=final)
                if final:
                    ins.then_inc((gate_done, up_done)[m], 1)

            def logits(g):
                pe.wait_ge(xt_lo_made, 2 * (g.n + 2) + 2)
                at_least(pe, expn_made, g.n)
                for h in range(HB):
                    for part in (xt_hi, xt_lo):
                        ins = pe.matmul(plog[:], router[:, h, :], part[g.b][:, h, :],
                                        start=(h == 0 and part is xt_hi),
                                        stop=(h == HB - 1 and part is xt_lo))
                ins.then_inc(logits_t_done, 1)

            def fold_logits(g):
                pe.wait_ge(logits_t_made, g.n + 1)
                for j in range(J):
                    ins = pe.matmul(plog[:, j * E:(j + 1) * E], logits_t[:, j * P:(j + 1) * P], fold[:],
                                    start=True, stop=True)
                ins.then_inc(logits_done, 1)

            def positions(g, psum=ppos[:, 0:J * E]):
                pe.wait_ge(chosen_made, g.n + 1)
                pe.wait_ge(norm_row_made, g.n + 2)
                at_least(pe, slots_made, g.n)
                pos = psum.rearrange("p (j e) -> p j e", j=J)
                pe.matmul(pos, before[:], chosen[:], start=True, stop=False)
                for k in range(1, J):
                    pe.matmul(pos[:, k:, :], ones[:], chosen[:, 0:J - k, :], start=False, stop=False)
                pe.matmul(pos, ones[:], earlier[g.b][:].unsqueeze(1).to_broadcast([P, J, E]), start=False,
                          stop=True).then_inc(pos_done, 1)

            def attention(g, j):
                at = slice(j * P, (j + 1) * P)
                pe.wait_ge(feat_lo_made, HB * (g.n + 2))
                pe.wait_ge(out_free, J * g.n + j + 1)
                products(pout[j % 2], [(feat_hi[:, r, at], feat_lo[:, r, at], wt_hi[:, r, :], wt_lo[:, r, :])
                                          for r in range(HB)], final=False)

            def shared_down(g, j):
                at = slice(j * P, (j + 1) * P)
                pe.wait_ge(hid_lo_made, IB * (g.n + 1))
                products(pout[j % 2], [(shid_hi[:, i, at], shid_lo[:, i, at], sdn_hi[:, i * H:(i + 1) * H],
                                           sdn_lo[:, i * H:(i + 1) * H]) for i in range(IB)],
                         first=False).then_inc(out_done, 1)

            def output(g, j):
                attention(g, j)
                shared_down(g, j)

            def group(g):
                nxt = g.next()
                first = isinstance(g.n, int) and g.n == 0
                dense_dots(g, range(1 if first else 0, HB))
                pe.wait_ge(xn_made, nxt.n + 1)
                pe.wait_ge(norm3_made, nxt.n + 2)
                turn_half(nxt.n + 2, xn, 0)
                if first:
                    pe.wait_ge(shared_lo_made, 1)
                shared_products(g, 0, 0)
                if first:
                    pe.wait_ge(norm_row_made, 2)
                else:
                    pe.wait_ge(slots_made, nxt.n)
                turn_half(nxt.n + 2, xn, 1, norm3)
                if first:
                    positions(g, pout[1][:, 0:J * E])
                shared_products(g, 0, 1)
                logits(nxt)
                shared_products(g, 1, 0, (0, 1))
                fold_logits(nxt)
                shared_products(g, 1, 0, (2, 3))
                shared_products(g, 1, 1)
                attention(g, 0)
                if first:
                    pe.wait_ge(slots_made, 1)
                attention(g, 1)
                positions(nxt)
                if first:
                    pe.wait_ge(shared_lo_made, 2)
                shared_down(g, 0)
                shared_down(g, 1)
                output(g, 2)
                output(g, 3)

            def last_group(g):
                dense_dots(g)
                for m in range(2):
                    shared_products(g, 0, m)
                attention(g, 0)
                for m in range(2):
                    shared_products(g, 1, m)
                attention(g, 1)
                shared_down(g, 0)
                shared_down(g, 1)
                output(g, 2)
                pe.wait_ge(slot_rows_loaded, 16)
                pe.wait_ge(expn_made, GROUPS)
                pe.transpose(plog[:, 0:P], slot_rows, ident[:]).then_inc(slot_rows_turned, 1)
                attention(g, 3)

            pe.wait_ge(ident_made, 1)
            pe.wait_ge(xis_loaded, 16)
            pe.transpose(ppos[:, 0:HB], xis_row[:], ident[0:HB, 0:HB]).then_inc(xis_turned, 1)
            pe.wait_ge(proj_loaded[0], 16)
            turn_half(0, xbuf[1], 0, free=0)
            pe.wait_ge(proj_loaded[1], 16)
            turn_half(0, xbuf[1], 1, psum=pmm2, free=0)
            pe.wait_ge(corr3_made, 1)
            for r in range(HB):
                ins = pe.transpose(ppos[0:3, r * P:(r + 1) * P], corr3[:, r, :], ident[:])
            ins.then_inc(corr_turned, 1)
            pe.wait_ge(iw_loaded[0], 16)
            turn_half(1, iw_raw, 0, psum=pout2, free=0)
            pe.wait_ge(iw_loaded[1], 16)
            turn_half(1, iw_raw, 1, free=1)
            pe.wait_ge(xt_lo_made, 3)
            projected(0, xt_hi[1], xt_lo[1], (0, 1))
            pe.wait_ge(xt_lo_made, 4)
            projected(0, xt_hi[1], xt_lo[1], (2, 3))
            pe.wait_ge(norm3_made, 1)
            pe.wait_ge(corr_row_made, 1)
            turn_small(norm3).then_inc(iw_norm_turned, 1)
            projected(1, xt_hi[1], xt_lo[1])
            pe.wait_ge(norm_row_made, 1)
            for r in range(2):
                less_norm(r, norm_row[1])
            for r in range(2, HB):
                pe.wait_ge(exp_done, r - 1)
                if r == HB - 1:
                    pe.wait_ge(xn_made, 1)
                    turn_half(2, xn, 0, psum=pout2, free=3)
                    pe.wait_ge(norm3_made, 2)
                    turn_half(2, xn, 1, norm3, free=4)
                dots(0, r, xt_hi[1], xt_lo[1], norm_row[1])
            pe.wait_ge(router_made, 1)
            logits(turn(0))
            dense_dots(turn(0), (0,))
            pe.wait_ge(consts_made, 1)
            fold_logits(turn(0))
            group(turn(0))
            group(turn(1))
            with pe.Fori(1, GROUPS // 2 - 1) as i:
                for b in range(2):
                    group(Turn(i, b))
            group(turn(GROUPS - 2))
            last_group(turn(GROUPS - 1))

            def e_turn(e):
                pe.wait_ge(gathered[e.b], 16 * CB * (e.i + 1))
                at_least(pe, e_xt_lo_made, e.n)
                for h in range(HB):
                    for c in range(CB):
                        ins = pe.transpose(ptr_e[:, h, c * P:(c + 1) * P], xe[e.b][:, c, h * P:(h + 1) * P],
                                           ident[:])
                ins.then_inc(e_turned, 1)

            def e_gate_up(e, parts=(0, 1)):
                pe.wait_ge(e_xt_lo_made, e.n + 1)
                pe.wait_ge(egu_lo_made, e.n + 1)
                at_least(pe, e_hid_made, e.n)
                for m in parts:
                    for i in range(IB):
                        at = [slice(m * HB * I + h * I + i * P, m * HB * I + h * I + (i + 1) * P)
                              for h in range(HB)]
                        ins = products(pmm[m][:, i * CAP:(i + 1) * CAP], [
                            (egu_hi[e.b][:, at[h]], egu_lo[e.b][:, at[h]], xt_hi[e.b][:, h, 0:CAP],
                             xt_lo[e.b][:, h, 0:CAP]) for h in range(HB)])
                    ins.then_inc((e_gate_done, e_up_done)[m], 1)

            def e_down(e):
                pe.wait_ge(e_hid_lo_made, e.n + 1)
                pe.wait_ge(edn_lo_made, e.n + 1)
                for c in range(CB):
                    at_least(pe, e_out_made, CB * (e.n - 1) + c + 1)
                    at = slice(c * P, (c + 1) * P)
                    products(pout[c], [
                        (hid_hi[:, e.b, i, at], hid_lo[:, e.b, i, at], edn_hi[e.b][:, i * H:(i + 1) * H],
                         edn_lo[e.b][:, i * H:(i + 1) * H]) for i in range(IB)]).then_inc(down_done, 1)

            e_turn(turn(0))
            shared_down(turn(GROUPS - 1), 3)
            e_gate_up(turn(0), (0,))
            e_turn(turn(1))
            e_gate_up(turn(0), (1,))
            pe.wait_ge(out_free, 2 + J * GROUPS)
            e_turn(turn(2))
            e_gate_up(turn(1))
            e_down(turn(0))
            with pe.Fori(1, E // 2 - 2, 2) as i:
                for k in range(4):
                    e = four(i, k)
                    e_turn(e.next())
                    e_gate_up(e)
                    e_down(e.prev())
            e_turn(turn(E - 1))
            e_gate_up(turn(E - 2))
            e_down(turn(E - 3))
            e_gate_up(turn(E - 1))
            e_down(turn(E - 2))
            e_down(turn(E - 1))

        @block.gpsimd
        def _(pool):
            steps = [0]

            def step(ins):
                ins.then_inc(pool_step, 1)
                steps[0] += 1

            def wait_apart(sem, value, sink=pool_sink):
                pool.wait_ge(sem, value)
                pool.tensor_tensor(sink[:], pool_carrier[:], pool_carrier[:], ALU.add)

            step(pool.memset(ident[:], 0.0))
            pool.wait_ge(pool_step, steps[0])
            pool.affine_select(out=ident[:], in_=ident[:], compare_op=ALU.not_equal, fill=1.0, base=0,
                               pattern=[[-1, P]], channel_multiplier=1).then_inc(ident_made, 1)
            step(pool.memset(pool_carrier[:], 0.0))
            step(pool.memset(before[:], 1.0))
            step(pool.memset(ones[:], 1.0))
            step(pool.memset(lower[:], 1.0))
            step(pool.memset(zeros, 0.0))
            step(pool.iota(token_ids_i[:], [[P, GROUPS * J]], base=0, channel_multiplier=1))
            step(pool.iota(no_token_i, [[1, CAP]], base=TOKENS, channel_multiplier=0))
            step(pool.iota(expert_base_i[:], [[-CAP, E]], base=OUTSIDE, channel_multiplier=0))
            pool.wait_ge(pool_step, steps[0])
            step(pool.affine_select(out=before[:], in_=before[:], compare_op=ALU.is_gt, fill=0.0, base=0,
                                    pattern=[[1, P]], channel_multiplier=-1))
            step(pool.affine_select(out=lower[:], in_=lower[:], compare_op=ALU.is_gt, fill=0.0, base=0,
                                    pattern=[[1, RG], [-1, RG]], channel_multiplier=0))
            step(pool.tensor_copy(token_ids[:], token_ids_i[:]))
            pool.wait_ge(ident_made, 1)
            step(pool.tensor_tensor(fold[:], ident[:, 0:E], ident[:, E:], ALU.add))
            step(pool.tensor_copy(no_token, no_token_i))
            pool.wait_ge(pool_step, steps[0])
            pool.tensor_copy(expert_base[:], expert_base_i[:]).then_inc(consts_made, 1)

            pool.wait_ge(shared_hi_made, 1)
            pool.tensor_tensor(sgu_lo[:], raw[0][:, 0:GU], sgu_hi[:].bitcast(F32), ALU.subtract).then_inc(
                shared_lo_made, 1)
            pool.wait_ge(shared_hi_made, 2)
            pool.tensor_tensor(sdn_lo[:], raw[0][:, GU:], sdn_hi[:].bitcast(F32), ALU.subtract).then_inc(
                shared_lo_made, 1)
            pool.wait_ge(table_made, 16 * (1 + 2 * SPARE // P))
            last_slot = pool.to_reg(SLOTS - 1)
            last_row = pool.to_reg(TOKENS + SPARE - 1)
            with pool.Fori(0, GROUPS // 2) as i:
                for b in range(2):
                    g = Turn(i, b)
                    pool.wait_ge(slots_made, g.n + 1)
                    pool.tensor_copy(ids[b][:], token_ids[:, bass.ds(J * g.n, J)]).then_inc(idx_copied, 1)
                    wait_apart(idx_copied, g.n + 1)
                    for j in range(J):
                        for k in range(K):
                            pool.indirect_dma_start(
                                out=slot_token, out_offset=bass.IndirectOffsetOnAxis(
                                    ap=slots[b][:, j, k:k + 1], axis=0),
                                in_=ids[b][:, j:j + 1], in_offset=None, bounds_check=last_slot,
                                oob_is_err=False).then_inc(scattered[b], 16)

            def gather(e, copied):
                pool.tensor_copy(gidx[e.b][:], slot_cols[:, bass.ds(CB * e.n, CB)]).then_inc(idx_copied, 1)
                wait_apart(idx_copied, copied)
                for c in range(CB):
                    pool.indirect_dma_start(
                        out=xe[e.b][:, c, :], out_offset=None, in_=rows,
                        in_offset=bass.IndirectOffsetOnAxis(ap=gidx[e.b][:, c:c + 1], axis=0),
                        bounds_check=last_row, oob_is_err=True).then_inc(gathered[e.b], 16)

            def add_rows(e, copied, last=False):
                at_least(pool, added, 16 * CB * e.n)
                if not last:
                    pool.wait_ge(e_out_made, CB * (e.n + 1))
                pool.tensor_copy(sidx[e.b][:], slot_cols[:, bass.ds(CB * e.n, CB)]).then_inc(idx_copied, 1)
                wait_apart(idx_copied, copied)
                for c in range(CB):
                    if last:
                        pool.wait_ge(e_out_made, CB * e.n + c + 1)
                    pool.indirect_dma_start(
                        out=out, out_offset=bass.IndirectOffsetOnAxis(ap=sidx[e.b][:, c:c + 1], axis=0),
                        in_=outs[e.b][:, c, :], in_offset=None, bounds_check=last_row,
                        oob_is_err=True, compute_op=ALU.add).then_inc(added, 16)

            pool.wait_ge(slot_cols_made, 1)
            pool.wait_ge(xn_stored, 16 * GROUPS)
            pool.wait_ge(w_stored, 16 * GROUPS)
            gather(turn(0), GROUPS + 1)
            gather(turn(1), GROUPS + 2)
            for n in range(2):
                pool.wait_ge(slot_w_made, n + 1)
                gather(turn(n + 2), GROUPS + n + 3)
            for b in range(2):
                pool.wait_ge(out_stored[b], 16 * GROUPS)

            def stage(e):
                wait_apart(slot_w_made, e.n + 2, pool_sink2)
                nxt = e.next()
                gather(Turn(nxt.i + 1, nxt.b), GROUPS + 2 * e.n + 3)
                add_rows(e.prev(), GROUPS + 2 * e.n + 4)

            with pool.Fori(1, E // 2 - 2, 2) as i:
                for k in range(4):
                    stage(four(i, k).prev())
            for n in range(E - 4, E):
                add_rows(turn(n), GROUPS + E + n + 1, last=n == E - 1)
            pool.wait_ge(added, 16 * CB * E)


_INS = ['L0_attn_x', 'L0_attn_input_weights', 'L0_attn_xis', 'L0_attn_proj_matrix', 'L0_ffn_router_w',
        'L0_ffn_gate_w', 'L0_ffn_up_w', 'L0_ffn_down_w', 'L0_ffn_shared_gate_w', 'L0_ffn_shared_up_w',
        'L0_ffn_shared_down_w']


def kernel(**inputs):
    import numpy as _np
    import concourse.bacc as _bacc
    from concourse import mybir as _mybir
    from concourse.bass_utils import run_bass_kernel_spmd as _run

    nc = _bacc.Bacc("TRN2", target_bir_lowering=False, num_devices=1)
    arrays, args = {}, []
    for name in _INS:
        a = _np.ascontiguousarray(inputs[name])
        arrays[f"in_{name}_dram"] = a
        args.append(nc.dram_tensor(f"in_{name}_dram", a.shape, _mybir.dt.from_np(a.dtype), kind="ExternalInput").ap())
    args.append(nc.dram_tensor("out_0_dram", (TOKENS + SPARE, H), _mybir.dt.from_np(_np.dtype("float32")),
                               kind="ExternalOutput").ap())
    build(nc, *args)
    r = _run(nc, [arrays], core_ids=[0])
    return r.results[0]["out_0_dram"][:TOKENS].reshape(4, 2048, H)
```
